# Optimizing a Trainium2 kernel written in Bass

```python
import numpy as np
import jax
import jax.numpy as jnp

def _softmax(x, axis=-1):
    return jax.nn.softmax(x, axis=axis)

def _gelu(x):
    return jax.nn.gelu(x, approximate=True)

def _silu(x):
    return jax.nn.silu(x)

def _sigmoid(x):
    return jax.nn.sigmoid(x)

def _layernorm(x, axis=-1, eps=1e-05):
    m = jnp.mean(x, axis=axis, keepdims=True)
    v = jnp.var(x, axis=axis, keepdims=True)
    return (x - m) / jnp.sqrt(v + eps)

def _scatter_add(tgt, idx, src, axis=0):
    return tgt.at[idx].add(src)

def _segment_sum(src, seg, n):
    return jax.ops.segment_sum(src, seg, n)
kernel_name = 'mk_conv_preact_d1_conv_nchw64_r2_aed84a'

def setup_inputs(seed: int=0):
    np.random.seed(seed)
    _w = jnp.asarray

    def _rec_inputs():
        import jax
        import jax.numpy as jnp
        _gk = jax.random.key(seed)
        x = 7.22e-05 + 1 * jax.random.normal(jax.random.fold_in(_gk, 1), (8, 32, 64, 64), jnp.float32)
        return x
    x = _rec_inputs()

    def _L0_conv_setup():
        import jax, jax.numpy as jnp
        import numpy as np
        K = 3
        PAD = K // 2
        IN_C = 32
        OUT_C = 32
        B, H, W = (8, 64, 64)

        def _conv2d(x, w, b, pad):
            out = jax.lax.conv_general_dilated(x, w, window_strides=(1, 1), padding=[(pad, pad), (pad, pad)], dimension_numbers=('NCHW', 'OIHW', 'NCHW'))
            return out + b[None, :, None, None]

        def _deconv2d(x, w, b):
            w2 = jnp.flip(w, axis=(-2, -1)).transpose(1, 0, 2, 3)
            return _conv2d(x, w2, b, K - 1 - 1)

        def _bilinear_sample(x, py, px):
            Hh, Ww = (x.shape[-2], x.shape[-1])
            y0 = jnp.floor(py)
            x0 = jnp.floor(px)
            out = jnp.zeros((x.shape[0],) + py.shape, dtype=x.dtype)
            for dy in (0.0, 1.0):
                for dx in (0.0, 1.0):
                    yi = y0 + dy
                    xi = x0 + dx
                    wy = 1.0 - jnp.abs(py - yi)
                    wx = 1.0 - jnp.abs(px - xi)
                    valid = (yi >= 0) & (yi < Hh) & (xi >= 0) & (xi < Ww)
                    yc = jnp.clip(yi, 0, Hh - 1).astype(jnp.int32)
                    xc = jnp.clip(xi, 0, Ww - 1).astype(jnp.int32)
                    v = x[:, yc, xc]
                    out = out + v * (wy * wx * valid.astype(x.dtype))[None]
            return out

        def _deform_conv2d(x, offset, w, b):
            Bn, C, Hh, Ww = x.shape
            off = offset.reshape(Bn, K * K, 2, Hh, Ww)
            ky, kx = jnp.meshgrid(jnp.arange(K), jnp.arange(K), indexing='ij')
            base_y = (jnp.arange(Hh) - PAD)[None, :, None] + ky.reshape(-1, 1, 1)
            base_x = (jnp.arange(Ww) - PAD)[None, None, :] + kx.reshape(-1, 1, 1)
            py = base_y.astype(x.dtype) + off[:, :, 0]
            px = base_x.astype(x.dtype) + off[:, :, 1]
            sampled = jax.vmap(_bilinear_sample)(x, py, px)
            wk = w.reshape(w.shape[0], w.shape[1], -1)
            return jnp.einsum('bckhw,ock->bohw', sampled, wk) + b[None, :, None, None]

        def _block(x, dc_w, dc_b, of_w, of_b, dw, db):
            h = jax.nn.relu(_deconv2d(x, dc_w, dc_b))
            offset = _conv2d(h, of_w, of_b, PAD)
            return jax.nn.relu(_deform_conv2d(h, offset, dw, db))
        key = jax.random.key(seed)
        ks = jax.random.split(key, 8)
        s = 0.05
        return {'x': jax.random.normal(ks[0], (B, IN_C, H, W), jnp.float32), 'deconv_w': jax.random.normal(ks[1], (4, IN_C, 32, K, K), jnp.float32) * s, 'deconv_b': jnp.zeros((4, 32), jnp.float32), 'off_w': jax.random.normal(ks[2], (4, 2 * K * K, 32, K, K), jnp.float32) * s, 'off_b': jnp.zeros((4, 2 * K * K), jnp.float32), 'dcn_w': jax.random.normal(ks[3], (4, IN_C, 32, K, K), jnp.float32) * s, 'dcn_b': jnp.zeros((4, IN_C), jnp.float32), 'fin_off_w': jax.random.normal(ks[4], (2 * K * K, 2 * IN_C, K, K), jnp.float32) * s, 'fin_off_b': jnp.zeros((2 * K * K,), jnp.float32), 'fin_dcn_w': jax.random.normal(ks[5], (OUT_C, 2 * IN_C, K, K), jnp.float32) * s, 'fin_dcn_b': jnp.zeros((OUT_C,), jnp.float32)}
    _L0_conv_all = _L0_conv_setup()
    _L0_conv_in = {k: v for k, v in _L0_conv_all.items() if k in ('deconv_w', 'deconv_b', 'off_w', 'off_b', 'dcn_w', 'dcn_b', 'fin_off_w', 'fin_off_b', 'fin_dcn_w', 'fin_dcn_b')}
    del _L0_conv_all
    return {'x': x, 'L0_conv_deconv_w': _L0_conv_in['deconv_w'], 'L0_conv_deconv_b': _L0_conv_in['deconv_b'], 'L0_conv_off_w': _L0_conv_in['off_w'], 'L0_conv_off_b': _L0_conv_in['off_b'], 'L0_conv_dcn_w': _L0_conv_in['dcn_w'], 'L0_conv_dcn_b': _L0_conv_in['dcn_b'], 'L0_conv_fin_off_w': _L0_conv_in['fin_off_w'], 'L0_conv_fin_off_b': _L0_conv_in['fin_off_b'], 'L0_conv_fin_dcn_w': _L0_conv_in['fin_dcn_w'], 'L0_conv_fin_dcn_b': _L0_conv_in['fin_dcn_b']}

def reference(x, L0_conv_deconv_w, L0_conv_deconv_b, L0_conv_off_w, L0_conv_off_b, L0_conv_dcn_w, L0_conv_dcn_b, L0_conv_fin_off_w, L0_conv_fin_off_b, L0_conv_fin_dcn_w, L0_conv_fin_dcn_b):
    import jax
    import jax.numpy as jnp

    def _L0_conv_ref(x, deconv_w, deconv_b, off_w, off_b, dcn_w, dcn_b, fin_off_w, fin_off_b, fin_dcn_w, fin_dcn_b):
        import jax, jax.numpy as jnp
        import numpy as np
        K = 3
        PAD = K // 2
        IN_C = 32
        OUT_C = 32
        B, H, W = (8, 64, 64)

        def _conv2d(x, w, b, pad):
            out = jax.lax.conv_general_dilated(x, w, window_strides=(1, 1), padding=[(pad, pad), (pad, pad)], dimension_numbers=('NCHW', 'OIHW', 'NCHW'))
            return out + b[None, :, None, None]

        def _deconv2d(x, w, b):
            w2 = jnp.flip(w, axis=(-2, -1)).transpose(1, 0, 2, 3)
            return _conv2d(x, w2, b, K - 1 - 1)

        def _bilinear_sample(x, py, px):
            Hh, Ww = (x.shape[-2], x.shape[-1])
            y0 = jnp.floor(py)
            x0 = jnp.floor(px)
            out = jnp.zeros((x.shape[0],) + py.shape, dtype=x.dtype)
            for dy in (0.0, 1.0):
                for dx in (0.0, 1.0):
                    yi = y0 + dy
                    xi = x0 + dx
                    wy = 1.0 - jnp.abs(py - yi)
                    wx = 1.0 - jnp.abs(px - xi)
                    valid = (yi >= 0) & (yi < Hh) & (xi >= 0) & (xi < Ww)
                    yc = jnp.clip(yi, 0, Hh - 1).astype(jnp.int32)
                    xc = jnp.clip(xi, 0, Ww - 1).astype(jnp.int32)
                    v = x[:, yc, xc]
                    out = out + v * (wy * wx * valid.astype(x.dtype))[None]
            return out

        def _deform_conv2d(x, offset, w, b):
            Bn, C, Hh, Ww = x.shape
            off = offset.reshape(Bn, K * K, 2, Hh, Ww)
            ky, kx = jnp.meshgrid(jnp.arange(K), jnp.arange(K), indexing='ij')
            base_y = (jnp.arange(Hh) - PAD)[None, :, None] + ky.reshape(-1, 1, 1)
            base_x = (jnp.arange(Ww) - PAD)[None, None, :] + kx.reshape(-1, 1, 1)
            py = base_y.astype(x.dtype) + off[:, :, 0]
            px = base_x.astype(x.dtype) + off[:, :, 1]
            sampled = jax.vmap(_bilinear_sample)(x, py, px)
            wk = w.reshape(w.shape[0], w.shape[1], -1)
            return jnp.einsum('bckhw,ock->bohw', sampled, wk) + b[None, :, None, None]

        def _block(x, dc_w, dc_b, of_w, of_b, dw, db):
            h = jax.nn.relu(_deconv2d(x, dc_w, dc_b))
            offset = _conv2d(h, of_w, of_b, PAD)
            return jax.nn.relu(_deform_conv2d(h, offset, dw, db))
        in_module = x
        x = _block(x, deconv_w[0], deconv_b[0], off_w[0], off_b[0], dcn_w[0], dcn_b[0])
        in_prev = jnp.zeros_like(x)
        for i in range(1, 4):
            in_cur = x + in_prev
            x = _block(in_cur, deconv_w[i], deconv_b[i], off_w[i], off_b[i], dcn_w[i], dcn_b[i])
            in_prev = in_cur
        x_cat = jnp.concatenate((x, in_module), axis=1)
        offset = _conv2d(x_cat, fin_off_w, fin_off_b, PAD)
        return _deform_conv2d(x_cat, offset, fin_dcn_w, fin_dcn_b)

    def _gn(v, G=32, eps=1e-05):
        B_, C_, H_, W_ = v.shape
        g = v.reshape(B_, G, C_ // G, H_, W_)
        m = jnp.mean(g, axis=(2, 3, 4), keepdims=True)
        s = jnp.var(g, axis=(2, 3, 4), keepdims=True)
        return ((g - m) / jnp.sqrt(s + eps)).reshape(v.shape)

    def _ln_c(v, eps=1e-06):
        m = jnp.mean(v, axis=1, keepdims=True)
        s = jnp.var(v, axis=1, keepdims=True)
        return (v - m) / jnp.sqrt(s + eps)

    def _ln_t(v, eps=1e-05):
        m = jnp.mean(v, axis=-1, keepdims=True)
        s = jnp.var(v, axis=-1, keepdims=True)
        return (v - m) / jnp.sqrt(s + eps)

    def _to_tokens(v):
        B_, C_, H_, W_ = v.shape
        return v.reshape(B_, C_, H_ * W_).transpose(0, 2, 1)

    def _from_tokens(t, like):
        B_, C_, H_, W_ = like.shape
        return t.transpose(0, 2, 1).reshape(B_, C_, H_, W_)
    x = x + _L0_conv_ref(_gn(x), L0_conv_deconv_w, L0_conv_deconv_b, L0_conv_off_w, L0_conv_off_b, L0_conv_dcn_w, L0_conv_dcn_b, L0_conv_fin_off_w, L0_conv_fin_off_b, L0_conv_fin_dcn_w, L0_conv_fin_dcn_b)
    return x

_drawn_inputs = setup_inputs


def setup_inputs(seed=0):
    import zlib

    import numpy as np

    out = dict(_drawn_inputs(seed))
    spreads = {'L0_conv_deconv_b': (0.0, 0.1),
     'L0_conv_off_b': (0.0, 0.378),
     'L0_conv_dcn_b': (0.0, 0.1),
     'L0_conv_fin_off_b': (0.0, 0.1),
     'L0_conv_fin_dcn_b': (0.0, 0.1)}
    factors = {}
    for name, (base, spread) in spreads.items():
        noise = np.random.default_rng([zlib.crc32(name.encode()), seed]).standard_normal(out[name].shape)
        drawn = base * np.exp(spread * noise) if base else spread * noise
        out[name] = jnp.asarray(drawn.astype(out[name].dtype))
    for name, factor in factors.items():
        out[name] = (out[name] * factor).astype(out[name].dtype)
    return out
```

```python
import concourse.bass as bass
import numpy as np
from concourse import mybir
from contextlib import ExitStack

ACT = mybir.ActivationFunctionType
ALU = mybir.AluOpType
AX = mybir.AxisListType
F32 = mybir.dt.float32
BF16 = mybir.dt.bfloat16
I32 = mybir.dt.int32

LAYERS = 4
GROUPS = 2
IMG = 4
CH = 32
SIDE = 64
TAPS = 9
PIX = SIDE * SIDE
XP = SIDE + 2
XSIZE = XP * XP
MARGIN = 6
HP = SIDE + 2 * MARGIN
HSIZE = HP * HP
BLK = 4
BPIX = BLK * BLK
BIG = 128
NBIG = PIX // BIG
SPLIT_ROWS = 3 * TAPS
MAIN_ROWS = SPLIT_ROWS + 2
FULL_ROWS = MAIN_ROWS + 1
EPS = 1e-5
BOUND0, BOUND1 = 2.0, 5.0


class Shape:

    def __init__(self, kind, sources):
        self.kind, self.sources = kind, sources
        self.tiles = 1 if kind == 0 else 2
        self.margin = 3 if kind == 0 else MARGIN
        self.win = BLK + 2 * self.margin
        self.rows = self.win // self.tiles
        self.npos = self.rows * self.win
        self.cols = 32 if kind == 0 else 16
        self.px = BLK * self.cols
        self.chunks = PIX // self.px
        self.blocks = self.cols // BLK
        if kind == 0:
            self.groups = [4] * 9
        elif sources == 1:
            self.groups = [6] * 6
        else:
            self.groups = [8, 8, 8, 8, 4]
        self.starts = [sum(self.groups[:j]) for j in range(len(self.groups))]
        self.bank = max(self.groups) * self.px
        self.jobs = self.blocks * sources // 4
        self.parts = [(s, w) for s in range(sources) for w in range(0, self.blocks, 4)]
        order = []
        ngr = len(self.groups)
        for j in range(ngr):
            if j == ngr - 2:
                order.append(("deform", 0))
            order.append(("coord", j))
        order += [("window", j) for j in range(self.jobs)]
        self.order = order
        self.uses = len(order)
        assert self.uses % 2 == 0
        self.slot = {use: n for n, use in enumerate(order)}
        self.after = {}
        for n in range(len(self.parts)):
            self.after.setdefault(min(2 + n, ngr - 3), []).append(n)


def build(nc, t):
    ctx = ExitStack()
    with ctx:
        def sb(name, shape, dt=F32):
            return ctx.enter_context(nc.sbuf_tensor(name, shape, dt))

        def sem(name):
            return ctx.enter_context(nc.semaphore(name))

        gn_store = nc.dram_tensor("gn_store", (GROUPS, 128, PIX), F32)

        X = sb("X", [128, GROUPS * XSIZE + 8])
        H = sb("H", [128, 2 * HSIZE + 64])
        A = sb("A", [128, 2, 36 * BIG])
        VT = sb("VT", [128, 16, 128])
        WIN = sb("WIN", [128, 4 * 256])
        AXY = sb("AXY", [128, 2, 3 * 512])
        SMP0 = sb("SMP0", [128, 8 * 144])
        DW = sb("DW", [128, TAPS * 128])
        TMP = sb("TMP", [128, BIG])
        OYX = sb("OYX", [128, NBIG * 2 * BIG], BF16)
        OC = sb("OC", [2 * CH, 2, IMG * BIG], BF16)
        FOFF = VT[:, 0:4, :].rearrange("p a b -> p (a b)").rearrange("p (n a) -> p n a", n=2)
        RES1 = VT[:, 4:6, :].rearrange("p a b -> p (a b)")
        HI = VT[:, 6, :].bitcast(BF16)
        MID = VT[:, 7, :].bitcast(BF16)
        OW = sb("OW", [128, 2, 2, TAPS * 128])
        CW = sb("CW", [128, 2, TAPS * 128])
        SEL = sb("SEL", [128, 5, TAPS * 128], BF16)
        BASE = sb("BASE", [128, 2, BIG])
        BIAS = sb("BIAS", [128, 4])
        CONST = sb("CONST", [128, 8 + 4 + 2 * 16])
        MX = sb("MX", [128, NBIG + 8])
        FLAG = sb("FLAG", [128, 1], I32)
        IDENT = sb("IDENT", [128, 128])
        SMP = [SMP0, DW]
        P = [ctx.enter_context(nc.psum_tensor(f"P{i}", [128, 3, 512], F32)) for i in range(2)]
        PS = ctx.enter_context(nc.psum_tensor("PS", [128, 2, 512], F32))
        M1, M2, MDATA = CONST[:, 0:1], CONST[:, 1:2], CONST[:, 2:3]

        bar = sem("bar")
        passed = sem("passed")
        loaded = sem("loaded")
        weights_loaded = sem("weights_loaded")
        x_loaded = [sem(f"x_loaded{g}") for g in range(GROUPS)]
        gn_step = sem("gn_step")
        gn_done = sem("gn_done")
        gn_root = sem("gn_root")
        gn_stored = sem("gn_stored")
        final_loaded = sem("final_loaded")
        out_stored = sem("out_stored")
        base_built = sem("base_built")
        conv_full = sem("conv_full")
        conv_free = sem("conv_free")
        off_full = sem("off_full")
        off_free = sem("off_free")
        max_done = sem("max_done")
        split_step = sem("split_step")
        split_done = sem("split_done")
        flag_step = sem("flag_step")
        copied = sem("copied")
        oc_full = [sem(f"oc_full{i}") for i in range(2)]
        win_full = sem("win_full")
        ring_full = sem("ring_full")
        ring_free = sem("ring_free")
        clamp_done = sem("clamp_done")
        hats_full = sem("hats_full")
        smp_full = sem("smp_full")
        smp_free = sem("smp_free")
        res_done = sem("res_done")
        turn = sem("turn")
        stepwise = [conv_full, conv_free, off_full, off_free, max_done, split_step, split_done, flag_step, copied,
                    *oc_full, win_full, ring_full, ring_free, clamp_done, hats_full, smp_full, smp_free, res_done, turn]
        credit = [(conv_free, 2), (off_free, 2), (max_done, 2), (split_done, 2), (ring_free, 2), (smp_full, 1),
                  (smp_free, 1), (res_done, 1), (turn, 1)]

        def x_view(group, row, col, rows, cols):
            start = group * XSIZE + row * XP + col
            return X[:, bass.ds(start, rows * XP)].rearrange("p (r c) -> p r c", c=XP)[:, :, 0:cols]

        def h_view(source, row, col, rows, cols):
            start = source * HSIZE + (row + MARGIN) * HP + col + MARGIN
            return H[:, bass.ds(start, rows * HP)].rearrange("p (r c) -> p r c", c=HP)[:, :, 0:cols]

        def out_view(group, row, col, cols):
            start = group * XSIZE + row * SIDE + col
            return X[:, bass.ds(start, BLK * SIDE)].rearrange("p (r c) -> p r c", c=SIDE)[:, :, 0:cols]

        def place(sh, c):
            per_row = SIDE // sh.cols
            return (c // per_row) * BLK, (c % per_row) * sh.cols

        def win_view(sh, slot):
            size = sh.win * sh.win
            return WIN[:, slot * (128 if sh.kind == 0 else 256):][:, 0:size]

        def smp_px(source, first_block, blocks):
            return SMP[source][:, first_block * 144:(first_block + blocks) * 144]

        def wait_alone(eng, semaphore, value):
            eng.wait_ge(semaphore, value)
            eng.sem_inc(passed, 1)

        def barrier(eng, count):
            eng.drain().then_inc(bar, 1)
            wait_alone(eng, bar, 5 * (count + 1))

        def clear_step(eng, count, clears):
            barrier(eng, count)
            if clears:
                for s in stepwise:
                    eng.sem_clear(s)
                for s, n in credit:
                    eng.sem_inc(s, n)
            barrier(eng, count + 1)

        BARS = 4

        def each_step(eng, layer_start, step, clears=False):
            clear_step(eng, 0, clears)
            with eng.Fori(0, LAYERS) as layer:
                layer_start(layer, False)
                with eng.Fori(0, GROUPS) as group:
                    step(layer, group, 2 + BARS * (layer * GROUPS + group), False)
            layer_start(LAYERS, True)
            with eng.Fori(0, GROUPS) as group:
                step(LAYERS, group, 2 + BARS * (LAYERS * GROUPS + group), True)

        def sampling(eng, bar_count, final, body, fallback, clears=False):
            barrier(eng, bar_count)
            kind = eng.value_load(FLAG[0:1, 0:1], min_val=0, max_val=2)
            sources = 2 if final else 1
            with eng.If(kind < 1):
                body(Shape(0, sources))
            with eng.If(kind == 1):
                body(Shape(1, sources))
            with eng.If(kind > 1):
                fallback(Shape(1, sources))
            barrier(eng, bar_count + 1)
            clear_step(eng, bar_count + 2, clears)

        def chunk_loop(eng, sh, body, tail):
            body(0, 0, True, False)
            with eng.Fori(0, (sh.chunks - 2) // 2) as pair:
                body(2 * pair + 1, 1, False, False)
                body(2 * pair + 2, 0, False, False)
            body(sh.chunks - 1, 1, False, True)
            tail(sh.chunks)

        def turns(sh):
            n = 2
            ngr = len(sh.groups)
            T = dict(window=0, transpose=1, keep=2)
            n = 3
            for j in range(ngr):
                T["coord", j], T["abs", j], T["clamp", j], T["product", j] = n, n + 1, n + 2, n + 3
                if j == 0:
                    pass
                n += 4
            for s in range(sh.sources):
                T["sample", s], T["read", s], T["add", s] = n, n + 1, n + 2
                n += 3
            T["n"] = n
            return T

        WINDOWS = 16

        def turn_base(T, c, p=None):
            per_chunk = WINDOWS * T["n"] + 5
            return c * per_chunk + (2 if p is None else 2 + p * T["n"]) + 1

        block = ctx.enter_context(nc.Block())

        @block.sync
        def _(sp):
            for g in range(GROUPS):
                src = t["x"][IMG * g:IMG * (g + 1)].rearrange("b c h w -> (b c) (h w)")
                sp.dma_start(A[:, g, 0:PIX], src).then_inc(x_loaded[g], 16)
            sp.dma_start(SEL[:, :, :].rearrange("p a b -> p (a b)"), t["sel"]).then_inc(loaded, 16)
            sp.dma_start(CONST[:, :], t["consts"]).then_inc(loaded, 16)
            sp.dma_start(IDENT[:, :], t["ident"]).then_inc(loaded, 16)
            for g in range(GROUPS):
                sp.wait_ge(gn_done, g + 1)
                sp.dma_start(gn_store[g].rearrange("p (r c) -> p r c", c=SIDE),
                             x_view(g, 1, 1, SIDE, SIDE)).then_inc(gn_stored, 16)
            sp.wait_ge(gn_stored, 32)

            def pick(weights, layer):
                return weights[bass.ds(layer, 1)].rearrange("a c k o -> (a c) k o")

            def layer_start(layer, final):
                sp.dma_start(BASE[:, :, :].rearrange("p a b -> p (a b)"), t["basec"]).then_inc(weights_loaded, 16)
                if not final:
                    for i in range(IMG):
                        q = slice(CH * i, CH * (i + 1))
                        d = DW[q, :].rearrange("p (k o) -> p k o", k=TAPS)[:, :, q]
                        sp.dma_start(d, pick(t["dc_w"], layer)).then_inc(weights_loaded, 16)
                        for yx in range(2):
                            d = OW[q, 0, yx, :].rearrange("p (k o) -> p k o", k=TAPS)[:, :, q]
                            sp.dma_start(d, pick(t["off_w"][:, yx], layer)).then_inc(weights_loaded, 16)
                        d = CW[q, 0, :].rearrange("p (k o) -> p k o", k=TAPS)[:, :, q]
                        sp.dma_start(d, pick(t["dcn_w"], layer)).then_inc(weights_loaded, 16)
                    sp.dma_start(BIAS[:, :], t["bias"][bass.ds(layer, 1)].rearrange("a p c -> (a p) c")).then_inc(weights_loaded, 16)
                else:
                    for i in range(IMG):
                        q = slice(CH * i, CH * (i + 1))
                        for s in range(2):
                            for yx in range(2):
                                d = OW[q, s, yx, :].rearrange("p (k o) -> p k o", k=TAPS)[:, :, q]
                                sp.dma_start(d, t["fin_off_w"][s, yx]).then_inc(weights_loaded, 16)
                            d = CW[q, s, :].rearrange("p (k o) -> p k o", k=TAPS)[:, :, q]
                            sp.dma_start(d, t["fin_dcn_w"][s]).then_inc(weights_loaded, 16)
                    sp.dma_start(BIAS[:, :], t["bias"][LAYERS]).then_inc(weights_loaded, 16)

            def stage(sh, c, par):
                at = (c if sh.kind == 0 else c // 2) * 2 * BIG
                for img in range(IMG):
                    for yx in range(2):
                        sp.dma_start(OC[CH * yx:CH * (yx + 1), par, BIG * img:BIG * (img + 1)],
                                     OYX[CH * img:CH * (img + 1), bass.ds(at + BIG * yx, BIG)]).then_inc(oc_full[par], 16)

            def body_of(sh):
                coord_last = sh.slot["coord", len(sh.groups) - 1]

                def body(c, par, first, last):
                    if first:
                        stage(sh, 0, 0)
                        stage(sh, 1, 1)
                    elif not last:
                        sp.wait_ge(ring_full, (c - 1) * sh.uses + coord_last + 1)
                        stage(sh, c + 1, 1 - par)

                chunk_loop(sp, sh, body, lambda c: None)

            def fallback(sh):
                T = turns(sh)
                with sp.Fori(0, sh.chunks) as c:
                    sp.wait_ge(turn, turn_base(T, c) - 2)
                    stage(sh, c, 0)
                    sp.wait_ge(oc_full[0], 16 * 2 * IMG * (c + 1))
                    sp.sem_inc(turn, 1)

            def step(layer, group, bar_count, final):
                if final:
                    sp.dma_start(h_view(1, 0, 0, SIDE, SIDE),
                                 gn_store[bass.ds(group, 1)].rearrange("a p (r c) -> p (a r) c", c=SIDE)).then_inc(final_loaded, 16)
                    sp.wait_ge(copied, 1)
                    sp.dma_start(X[:, bass.ds(group * XSIZE, PIX)],
                                 t["x"][bass.ds(group * IMG, IMG)].rearrange("b c h w -> (b c) (h w)")).then_inc(final_loaded, 16)
                    wait_alone(sp, final_loaded, 32 * group + 32)
                sampling(sp, bar_count, final, body_of, fallback)
                if final:
                    sp.dma_start(t["out"][bass.ds(group * IMG, IMG)].rearrange("b c h w -> (b c) (h w)"),
                                 X[:, bass.ds(group * XSIZE, PIX)]).then_inc(out_stored, 16)

            each_step(sp, layer_start, step)
            sp.wait_ge(out_stored, 16 * GROUPS)

        N_LOADS = IMG * 4 + 2
        N_FINAL_LOADS = IMG * 6 + 2

        def wait_weights(eng, layer, final):
            if final:
                eng.wait_ge(weights_loaded, 16 * (LAYERS * N_LOADS + N_FINAL_LOADS))
            else:
                wait_alone(eng, weights_loaded, 16 * N_LOADS * (layer + 1))

        @block.tensor
        def _(pe):
            def layer_start(layer, final):
                wait_weights(pe, layer, final)

            def first_conv(group):
                for i in range(SIDE // 8):
                    pe.wait_ge(conv_free, i + 1)
                    for k in range(TAPS):
                        mm = nc.tensor.matmul(P[0][:, i % 2, :], DW[:, 128 * k:128 * (k + 1)],
                                              x_view(group, i * 8 + k // 3, k % 3, 8, SIDE),
                                              start=k == 0, stop=k == TAPS - 1)
                    mm.then_inc(conv_full, 1)

            def offset_conv(sources):
                with pe.Fori(0, SIDE // BLK) as strip:
                    for par in range(2):
                        pe.wait_ge(off_free, 2 * strip + par + 1)
                        for yx in range(2):
                            for s in range(sources):
                                for k in range(TAPS):
                                    mm = nc.tensor.matmul(
                                        P[1][:, par, BIG * yx:BIG * (yx + 1)], OW[:, s, yx, 128 * k:128 * (k + 1)],
                                        h_view(s, strip * BLK + k // 3 - 1, 32 * par + k % 3 - 1, BLK, 32),
                                        start=s == 0 and k == 0, stop=s == sources - 1 and k == TAPS - 1)
                        mm.then_inc(off_full, 1)

            def coord(sh, j, slot, par, rows):
                for i in range(sh.groups[j]):
                    img, tap = divmod(sh.starts[j] + i, TAPS)
                    for n in range(sh.tiles + 1):
                        yx = 1 if n == sh.tiles else 0
                        q = CH * yx
                        table = n if sh.kind == 0 else 2 + n
                        off = OC[q:q + rows, par, BIG * img:BIG * (img + 1)]
                        if sh.kind:
                            off = off.rearrange("p (r h c) -> p h r c", r=BLK, h=2)[:, coord_half[0]]
                        mm = nc.tensor.matmul(P[slot][0:sh.npos, n, i * sh.px:(i + 1) * sh.px],
                                              SEL[q:q + rows, table, 128 * tap:128 * tap + sh.npos],
                                              off, start=True, stop=True)
                return mm

            coord_half = [0]

            def sample(sh, source, first, par, tile_of):
                for w in range(4):
                    out = PS[:, w // 2, 144 * (w % 2):144 * (w % 2) + 144]
                    for n in range(sh.tiles):
                        a = A[0:sh.npos, par, n * 36 * sh.px:(n + 1) * 36 * sh.px].rearrange(
                            "p (k y x) -> p k y x", k=36, y=BLK)
                        for img in range(IMG):
                            q = slice(CH * img, CH * (img + 1))
                            mm = nc.tensor.matmul(
                                out[q].rearrange("p (k y x) -> p k y x", k=TAPS, y=BLK),
                                VT[0:sh.npos, tile_of(source, first + w, n), q],
                                a[:, TAPS * img:TAPS * (img + 1), :, BLK * (first + w):BLK * (first + w + 1)],
                                start=n == 0, stop=n == sh.tiles - 1)
                return mm

            def deform(sh, slot):
                for s in range(sh.sources):
                    for k in range(TAPS):
                        rhs = smp_px(s, 0, sh.blocks).rearrange("p (w k a) -> p w k a", k=TAPS, a=BPIX)[:, :, k, :]
                        mm = nc.tensor.matmul(P[slot][:, 0, 0:sh.px], CW[:, s, 128 * k:128 * (k + 1)], rhs,
                                              start=s == 0 and k == 0, stop=s == sh.sources - 1 and k == TAPS - 1)
                return mm

            def transpose(sh, slot, i, n, column):
                return nc.tensor.transpose(P[slot][0:sh.npos, column // 4, 128 * (column % 4):128 * (column % 4) + 128],
                                           win_view(sh, i)[:, n * sh.npos:(n + 1) * sh.npos], IDENT[:, :])

            def body_of(sh):
                tile_of = lambda s, w, n: (s * sh.blocks + w) * sh.tiles + n

                def use(c, name, j=0):
                    n = sh.slot[name, j]
                    pe.wait_ge(ring_free, c * sh.uses + n + 1)
                    return n % 2

                def part(c, n, par):
                    pe.wait_ge(hats_full, (c + 1) * len(sh.groups))
                    pe.wait_ge(smp_free, c * len(sh.parts) + n + 1)
                    sample(sh, *sh.parts[n], par, tile_of).then_inc(smp_full, 1)

                def body(c, par, first, last):
                    pe.wait_ge(oc_full[par], 16 * 2 * IMG * (c // 2 + 1))
                    coord_half[0] = par
                    for j in range(len(sh.groups)):
                        if not first and ("deform", 0) == sh.order[sh.slot["coord", j] - 1]:
                            pe.wait_ge(smp_free, c * len(sh.parts) + 1)
                            slot = use(c, "deform")
                            deform(sh, slot).then_inc(ring_full, 1)
                        elif first and ("deform", 0) == sh.order[sh.slot["coord", j] - 1]:
                            use(c, "deform")
                            pe.drain().then_inc(ring_full, 1)
                        slot = use(c, "coord", j)
                        coord(sh, j, slot, par, MAIN_ROWS).then_inc(ring_full, 1)
                        if not first:
                            for n in sh.after.get(j, []):
                                part(c - 1, n, 1 - par)
                    for j in range(sh.jobs):
                        pe.wait_ge(win_full, c * sh.jobs + j + 1)
                        slot = use(c, "window", j)
                        for i in range(4):
                            ws = i + (4 * (j % 2) if sh.kind == 0 else 0)
                            for n in range(sh.tiles):
                                mm = transpose(sh, slot, ws, n, i * sh.tiles + n)
                        mm.then_inc(ring_full, 1)

                def tail(c):
                    pe.wait_ge(ring_free, c * sh.uses + 2)
                    for n in range(len(sh.parts)):
                        part(c - 1, n, 1)
                    pe.wait_ge(smp_free, c * len(sh.parts) + 1)
                    deform(sh, 0).then_inc(ring_full, 1)

                chunk_loop(pe, sh, body, tail)

            def fallback(sh):
                T = turns(sh)

                def chunk(c, par):
                    coord_half[0] = par
                    with pe.Fori(0, WINDOWS) as p:
                        base = turn_base(T, c, p)
                        pe.wait_ge(turn, base + T["transpose"])
                        for s in range(sh.sources):
                            for n in range(sh.tiles):
                                mm = transpose(sh, 0, s, n, s * sh.tiles + n)
                        mm.then_inc(turn, 1)
                        for j in range(len(sh.groups)):
                            pe.wait_ge(turn, base + T["coord", j])
                            coord(sh, j, 0, 0, FULL_ROWS).then_inc(turn, 1)
                        for s in range(sh.sources):
                            pe.wait_ge(turn, base + T["sample", s])
                            sample(sh, s, 0, 0, lambda s, w, n: s * sh.tiles + n).then_inc(turn, 1)
                    pe.wait_ge(turn, turn_base(T, c, WINDOWS))
                    deform_sum(sh).then_inc(turn, 1)

                def deform_sum(sh):
                    for s in range(sh.sources):
                        for k in range(TAPS):
                            rhs = smp_px(s, 4, 4).rearrange("p (w k a) -> p w k a", k=TAPS, a=BPIX)[:, :, k, :]
                            mm = nc.tensor.matmul(P[0][:, 0, 0:sh.px], CW[:, s, 128 * k:128 * (k + 1)], rhs,
                                                  start=s == 0 and k == 0, stop=s == sh.sources - 1 and k == TAPS - 1)
                    return mm

                with pe.Fori(0, sh.chunks // 2) as pair:
                    chunk(2 * pair, 0)
                    chunk(2 * pair + 1, 1)

            def step(layer, group, bar_count, final):
                if not final:
                    first_conv(group)
                    pe.wait_ge(conv_free, 8 + 2)
                else:
                    pe.wait_ge(copied, 1)
                    wait_alone(pe, final_loaded, 32 * group + 32)
                offset_conv(2 if final else 1)
                sampling(pe, bar_count, final, body_of, fallback)

            each_step(pe, layer_start, step)

        @block.scalar
        def _(act):
            for g in range(GROUPS):
                act.wait_ge(gn_step, 4 + 4 * g + 3)
                nc.scalar.activation(MX[:, 4 * g + 2:4 * g + 3], MX[:, 4 * g + 1:4 * g + 2], ACT.Sqrt).then_inc(gn_root, 1)

            def layer_start(layer, final):
                wait_weights(act, layer, final)

            def raster(sh, slot):
                return P[slot][:, 0, 0:sh.px].rearrange("p (w y x) -> p y w x", w=sh.blocks, y=BLK)

            def tmp_view(sh):
                return TMP[:, 0:sh.px].rearrange("p (y w x) -> p y w x", y=BLK, w=sh.blocks)

            def body_of(sh, final):
                ngr = len(sh.groups)

                def out_act(c, slot):
                    act.wait_ge(res_done, c + 1)
                    nc.scalar.activation(tmp_view(sh), raster(sh, slot), ACT.Identity if final else ACT.Relu,
                                         bias=BIAS[:, 1:2]).then_inc(ring_free, 1)

                def read_part(c, n):
                    s, w = sh.parts[n]
                    act.wait_ge(smp_full, c * len(sh.parts) + n + 2)
                    nc.scalar.activation(smp_px(s, w, 4).rearrange("p (a b) -> p a b", a=2), PS[:, :, 0:288],
                                         ACT.Copy).then_inc(smp_free, 1)

                def body(c, par, first, last):
                    for j in range(ngr):
                        if ("deform", 0) == sh.order[sh.slot["coord", j] - 1]:
                            n = sh.slot["deform", 0]
                            act.wait_ge(ring_full, c * sh.uses + n + 1)
                            if first:
                                act.drain().then_inc(ring_free, 1)
                            else:
                                out_act(c - 1, n % 2)
                        n = sh.slot["coord", j]
                        act.wait_ge(ring_full, c * sh.uses + n + 1)
                        if not (first and j < 2):
                            act.wait_ge(hats_full, c * ngr + j - 1)
                        size = sh.groups[j] * sh.px
                        buf = AXY[0:sh.npos, (par * ngr + j) % 2, 0:(sh.tiles + 1) * sh.bank].rearrange(
                            "p (n a) -> p n a", n=sh.tiles + 1)
                        nc.scalar.activation(buf[:, :, 0:size], P[n % 2][0:sh.npos, 0:sh.tiles + 1, 0:size],
                                             ACT.Abs).then_inc(ring_free, 1)
                        if not first:
                            for part in sh.after.get(j, []):
                                read_part(c - 1, part)
                    for j in range(sh.jobs):
                        n = sh.slot["window", j]
                        act.wait_ge(ring_full, c * sh.uses + n + 1)
                        count = 4 * sh.tiles
                        vt = VT[0:sh.npos, j * count:(j + 1) * count, :]
                        src = P[n % 2][0:sh.npos, 0:sh.tiles, :].rearrange("p a (b c) -> p (a b) c", c=128)
                        nc.scalar.activation(vt, src, ACT.Copy).then_inc(ring_free, 1)

                def tail(c):
                    for n in range(len(sh.parts)):
                        read_part(c - 1, n)
                    act.wait_ge(ring_full, c * sh.uses + 1)
                    out_act(c - 1, 0)

                chunk_loop(act, sh, body, tail)

            def fallback_of(sh, final):
                T = turns(sh)
                with act.Fori(0, sh.chunks) as c:
                    with act.Fori(0, WINDOWS) as p:
                        base = turn_base(T, c, p)
                        wait_alone(act, turn, base + T["keep"])
                        count = sh.sources * sh.tiles
                        nc.scalar.activation(VT[:, 0:count, :], P[0][:, 0, 0:128 * count].rearrange(
                            "p (a b) -> p a b", b=128), ACT.Copy).then_inc(turn, 1)
                        for j in range(len(sh.groups)):
                            wait_alone(act, turn, base + T["abs", j])
                            size = sh.groups[j] * sh.px
                            buf = AXY[:, 0, 0:3 * sh.bank].rearrange("p (n a) -> p n a", n=3)
                            nc.scalar.activation(buf[:, 0:2, 0:size], P[0][:, 0:2, 0:size], ACT.Abs,
                                                 bias=CONST[:, bass.ds(8 + p // 4, 1)])
                            nc.scalar.activation(buf[:, 2, 0:size], P[0][:, 2, 0:size], ACT.Abs,
                                                 bias=CONST[:, bass.ds(8 + p % 4, 1)]).then_inc(turn, 1)
                        for s in range(sh.sources):
                            wait_alone(act, turn, base + T["read", s])
                            nc.scalar.activation(smp_px(s, 0, 4).rearrange("p (a b) -> p a b", a=2), PS[:, :, 0:288],
                                                 ACT.Copy).then_inc(turn, 1)
                    wait_alone(act, turn, turn_base(T, c, WINDOWS) + 1)
                    nc.scalar.activation(tmp_view(sh), raster(sh, 0), ACT.Identity if final else ACT.Relu,
                                         bias=BIAS[:, 1:2]).then_inc(turn, 1)

            def step(layer, group, bar_count, final):
                if not final:
                    for i in range(SIDE // 8):
                        act.wait_ge(conv_full, i + 1)
                        nc.scalar.activation(h_view(0, i * 8, 0, 8, SIDE),
                                             P[0][:, i % 2, :].rearrange("p (r c) -> p r c", c=SIDE), ACT.Relu,
                                             bias=BIAS[:, 0:1]).then_inc(conv_free, 1)
                sampling(act, bar_count, final, lambda sh: body_of(sh, final), lambda sh: fallback_of(sh, final))

            each_step(act, layer_start, step)

        @block.vector
        def _(dve):
            nc.vector.memset(X[:, :], 0.0).then_inc(gn_step, 1)
            nc.vector.memset(DW[:, :], 0.0).then_inc(gn_step, 1)
            nc.vector.memset(OW[:, :, :, :], 0.0).then_inc(gn_step, 1)
            nc.vector.memset(CW[:, :, :], 0.0).then_inc(gn_step, 1)
            stats = AXY[:, 0, 0:48].rearrange("p (a b) -> p a b", b=6)
            for g in range(GROUPS):
                done = 4 + 4 * g
                dve.wait_ge(x_loaded[g], 16)
                dve.wait_ge(gn_step, done)
                for i in range(8):
                    last = nc.vector.bn_stats(stats[:, i, :], A[:, g, 512 * i:512 * (i + 1)])
                last.then_inc(gn_step, 1)
                dve.wait_ge(gn_step, done + 1)
                nc.vector.bn_aggr(MX[:, 4 * g:4 * g + 2], stats).then_inc(gn_step, 1)
                dve.wait_ge(gn_step, done + 2)
                nc.vector.tensor_scalar_add(MX[:, 4 * g + 1:4 * g + 2], MX[:, 4 * g + 1:4 * g + 2], EPS).then_inc(gn_step, 1)
                dve.wait_ge(gn_root, g + 1)
                nc.vector.reciprocal(MX[:, 4 * g + 3:4 * g + 4], MX[:, 4 * g + 2:4 * g + 3]).then_inc(gn_step, 1)
                dve.wait_ge(gn_step, done + 4)
                nc.vector.tensor_scalar(x_view(g, 1, 1, SIDE, SIDE), A[:, g, 0:PIX].rearrange("p (r c) -> p r c", c=SIDE),
                                        MX[:, 4 * g:4 * g + 1], MX[:, 4 * g + 3:4 * g + 4], ALU.subtract,
                                        ALU.mult).then_inc(gn_done, 1)
            dve.wait_ge(loaded, 48)

            def layer_start(layer, final):
                wait_weights(dve, layer, final)
                for yx in range(2):
                    nc.vector.tensor_scalar(BASE[:, yx, :], BASE[:, yx, :], BIAS[:, 2 + yx:3 + yx], None,
                                            ALU.add).then_inc(base_built, 1)
                wait_alone(dve, base_built, 2 * layer + 2)

            def residual(sh, layer, group, c, final):
                row, col = place(sh, c)
                tmp = TMP[:, 0:sh.px].rearrange("p (r c) -> p r c", r=BLK)
                if final:
                    dst = out_view(group, row, col, sh.cols)
                    flag = CONST[:, 7:8]
                else:
                    dst = x_view(group, row + 1, col + 1, BLK, sh.cols)
                    flag = CONST[:, bass.ds(3 + layer, 1)]
                return nc.vector.scalar_tensor_tensor(dst, dst, flag, tmp, ALU.mult, ALU.add)

            def product(sh, j, buf, par):
                size = sh.groups[j] * sh.px
                a = A[0:sh.npos, par, 0:sh.tiles * 36 * sh.px].rearrange("p (n a) -> p n a", n=sh.tiles)
                a = a[:, :, sh.starts[j] * sh.px:sh.starts[j] * sh.px + size]
                hx = buf[:, sh.tiles:sh.tiles + 1, 0:size]
                if sh.tiles > 1:
                    hx = hx.broadcast_to([sh.npos, sh.tiles, size])
                return nc.vector.tensor_tensor(a, buf[:, 0:sh.tiles, 0:size], hx, ALU.mult)

            def body_of(sh, layer, group, final):
                ngr = len(sh.groups)

                def body(c, par, first, last):
                    for j in range(ngr):
                        size = sh.groups[j] * sh.px
                        n = sh.slot["coord", j]
                        if not first and ("deform", 0) == sh.order[n - 1]:
                            dve.wait_ge(ring_free, c * sh.uses + n - 1 + 3)
                            residual(sh, layer, group, c - 1, final).then_inc(res_done, 1)
                        buf = AXY[0:sh.npos, (par * ngr + j) % 2, 0:(sh.tiles + 1) * sh.bank].rearrange(
                            "p (n a) -> p n a", n=sh.tiles + 1)
                        dve.wait_ge(ring_free, c * sh.uses + n + 3)
                        nc.vector.tensor_scalar(buf[:, :, 0:size], buf[:, :, 0:size], 1.0, 1.0, ALU.min,
                                                ALU.subtract).then_inc(clamp_done, 1)
                        dve.wait_ge(clamp_done, c * ngr + j + 1)
                        if not first and j == 0:
                            dve.wait_ge(smp_full, (c - 1) * len(sh.parts) + 1)
                        product(sh, j, buf, par).then_inc(hats_full, 1)

                def tail(c):
                    dve.wait_ge(ring_free, c * sh.uses + 3)
                    residual(sh, layer, group, c - 1, final).then_inc(res_done, 1)

                chunk_loop(dve, sh, body, tail)

            def fallback_of(sh, layer, group, final):
                T = turns(sh)
                with dve.Fori(0, sh.chunks) as c:
                    dve.wait_ge(turn, turn_base(T, c) - 1)
                    for s in range(sh.sources):
                        mm = nc.vector.memset(smp_px(s, 4, 4), 0.0)
                    mm.then_inc(turn, 1)
                    with dve.Fori(0, WINDOWS) as p:
                        base = turn_base(T, c, p)
                        for j in range(len(sh.groups)):
                            size = sh.groups[j] * sh.px
                            buf = AXY[:, 0, 0:3 * sh.bank].rearrange("p (n a) -> p n a", n=3)
                            dve.wait_ge(turn, base + T["clamp", j])
                            nc.vector.tensor_scalar(buf[:, :, 0:size], buf[:, :, 0:size], 1.0, 1.0, ALU.min,
                                                    ALU.subtract).then_inc(turn, 1)
                            dve.wait_ge(turn, base + T["product", j])
                            product(sh, j, buf, 0).then_inc(turn, 1)
                        for s in range(sh.sources):
                            dve.wait_ge(turn, base + T["add", s])
                            nc.vector.tensor_tensor(smp_px(s, 4, 4), smp_px(s, 4, 4), smp_px(s, 0, 4),
                                                    ALU.add).then_inc(turn, 1)
                    dve.wait_ge(turn, turn_base(T, c, WINDOWS) + 2)
                    residual(sh, layer, group, c, final).then_inc(turn, 1)

            def step(layer, group, bar_count, final):
                if final:
                    nc.vector.tensor_copy(h_view(0, 0, 0, SIDE, SIDE), x_view(group, 1, 1, SIDE, SIDE)).then_inc(copied, 1)
                with dve.Fori(0, SIDE // BLK) as strip:
                    for par in range(2):
                        c = 2 * strip + par
                        dve.wait_ge(off_full, c + 1)
                        dve.wait_ge(split_done, c + 1)
                        dve.wait_ge(max_done, c + 1)
                        for yx in range(2):
                            where = CONST[:, bass.ds(12 + strip, 1)] if yx == 0 else CONST[:, 28 + par:29 + par]
                            fo = nc.vector.scalar_tensor_tensor(FOFF[:, par, BIG * yx:BIG * (yx + 1)],
                                                                P[1][:, par, BIG * yx:BIG * (yx + 1)], where,
                                                                BASE[:, yx, :], ALU.add, ALU.add)
                        fo.then_inc(off_free, 1)
                        dve.wait_ge(off_free, c + 3)
                        nc.vector.tensor_reduce(MX[:, bass.ds(c, 1)], FOFF[:, par, :], AX.X, ALU.max,
                                                apply_absolute_value=True).then_inc(max_done, 1)
                dve.wait_ge(max_done, NBIG + 2)
                nc.vector.tensor_reduce(MX[:, NBIG:NBIG + 1], MX[:, 0:NBIG], AX.X, ALU.max).then_inc(flag_step, 1)
                dve.wait_ge(flag_step, 1)
                nc.vector.tensor_scalar(MX[:, NBIG + 1:NBIG + 2], MX[:, NBIG:NBIG + 1], MDATA, None, ALU.mult).then_inc(flag_step, 1)
                dve.wait_ge(flag_step, 3)
                nc.vector.tensor_scalar(MX[:, NBIG + 3:NBIG + 4], MX[:, NBIG + 2:NBIG + 3], BOUND0, None, ALU.is_ge).then_inc(flag_step, 1)
                nc.vector.tensor_scalar(MX[:, NBIG + 4:NBIG + 5], MX[:, NBIG + 2:NBIG + 3], BOUND1, None, ALU.is_ge).then_inc(flag_step, 1)
                dve.wait_ge(flag_step, 5)
                nc.vector.tensor_tensor(FLAG[:, :], MX[:, NBIG + 3:NBIG + 4], MX[:, NBIG + 4:NBIG + 5], ALU.add).then_inc(flag_step, 1)
                sampling(dve, bar_count, final, lambda sh: body_of(sh, layer, group, final),
                         lambda sh: fallback_of(sh, layer, group, final))

            each_step(dve, layer_start, step)

        @block.gpsimd
        def _(pool):
            nc.gpsimd.memset(H[:, :], 0.0)

            def body_of(sh):
                def body(c, par, first, last):
                    row, col = place(sh, c)
                    for j in range(sh.jobs):
                        back = 2 if sh.kind == 0 else 1
                        if j >= back:
                            pool.wait_ge(ring_full, c * sh.uses + sh.slot["window", j - back] + 1)
                        elif not first:
                            pool.wait_ge(ring_full, (c - 1) * sh.uses + sh.slot["window", sh.jobs + j - back] + 1)
                        for i in range(4):
                            s, w = divmod(4 * j + i, sh.blocks)
                            ws = i + (4 * (j % 2) if sh.kind == 0 else 0)
                            cp = nc.gpsimd.tensor_copy(
                                win_view(sh, ws).rearrange("p (r c) -> p r c", c=sh.win),
                                h_view(s, row - sh.margin, col + BLK * w - sh.margin, sh.win, sh.win))
                        cp.then_inc(win_full, 1)

                chunk_loop(pool, sh, body, lambda c: None)

            def fallback(sh):
                T = turns(sh)
                with pool.Fori(0, sh.chunks) as c:
                    with pool.Fori(0, WINDOWS) as p:
                        pool.wait_ge(turn, turn_base(T, c, p) + T["window"])
                        for s in range(sh.sources):
                            cp = nc.gpsimd.tensor_copy(win_view(sh, s).rearrange("p (r c) -> p r c", c=sh.win),
                                                       h_view(s, (p // 4) * 16, (p % 4) * 16, sh.win, sh.win))
                        cp.then_inc(turn, 1)

            def step(layer, group, bar_count, final):
                with pool.Fori(0, SIDE // BLK) as strip:
                    for par in range(2):
                        c = 2 * strip + par
                        wait_alone(pool, off_free, c + 3)
                        nc.gpsimd.tensor_scalar(HI[:, :], FOFF[:, par, :], M1, None, ALU.mult).then_inc(split_step, 1)
                        pool.wait_ge(split_step, 3 * c + 1)
                        nc.gpsimd.tensor_tensor(RES1[:, :], FOFF[:, par, :], HI[:, :], ALU.subtract).then_inc(split_step, 1)
                        wait_alone(pool, split_step, 3 * c + 2)
                        nc.gpsimd.tensor_scalar(MID[:, :], RES1[:, :], M2, None, ALU.mult).then_inc(split_step, 1)
                        pool.wait_ge(split_step, 3 * c + 3)
                        nc.gpsimd.tensor_tensor(OYX[:, bass.ds(c * 2 * BIG, 2 * BIG)], RES1[:, :], MID[:, :],
                                                ALU.subtract).then_inc(split_done, 1)
                        pool.wait_ge(split_done, c + 3)
                pool.wait_ge(flag_step, 2)
                nc.gpsimd.partition_all_reduce(MX[:, NBIG + 2:NBIG + 3], MX[:, NBIG + 1:NBIG + 2], 128,
                                               bass.bass_isa.ReduceOp.max).then_inc(flag_step, 1)
                sampling(pool, bar_count, final, body_of, fallback, clears=True)

            each_step(pool, lambda layer, final: None, step, clears=True)


def _tables():
    npos = {0: 100, 1: 128}
    sel = np.zeros((128, 5, TAPS, 128), np.float32)
    tables = [(0, 0, 0), (0, 1, 0), (1, 0, 0), (1, 0, 1), (1, 1, 0)]
    for n, (kind, yx, tile) in enumerate(tables):
        win, rows, margin = (10, 10, 3) if kind == 0 else (16, 8, 6)
        for q in range(0, 128, 32):
            for k in range(TAPS):
                for s in range(3):
                    sel[q + s * TAPS + k, n, k, :] = 1.0
                pos = np.arange(npos[kind])
                at = pos % win if yx else pos // win + rows * tile
                shift = (k % 3 if yx else k // 3) - 1
                sel[q + SPLIT_ROWS, n, k, :npos[kind]] = shift + margin - at
                sel[q + SPLIT_ROWS + 1, n, k, :] = 1.0
                sel[q + SPLIT_ROWS + 2, n, k, :] = 1.0
    base = np.zeros((128, 2, BLK, 32), np.float32)
    consts = np.zeros((128, 44), np.float32)
    for q in range(0, 128, 32):
        consts[q + TAPS:q + SPLIT_ROWS, 0] = 1.0
        consts[q + 2 * TAPS:q + SPLIT_ROWS, 1] = 1.0
        consts[q:q + SPLIT_ROWS, 2] = 1.0
        base[q + SPLIT_ROWS] = 1.0
        base[q + SPLIT_ROWS + 1, 0] = np.arange(BLK)[:, None]
        base[q + SPLIT_ROWS + 1, 1] = np.arange(32)[None, :] % BLK
        base[q + SPLIT_ROWS + 2, 1] = np.arange(32)[None, :] // BLK * BLK
        consts[q + SPLIT_ROWS + 2, 12:28] = np.arange(16) * BLK
        consts[q + SPLIT_ROWS + 2, 28:30] = [0.0, 32.0]
    consts[:, 3:8] = [0.0, 1.0, 1.0, 0.0, 1.0]
    consts[:, 8:12] = -6.0 - 16.0 * np.arange(4)
    return sel, base.reshape(128, 2 * BIG), consts, np.eye(128, dtype=np.float32)


def kernel(**inputs):
    import concourse.bacc as bacc
    import ml_dtypes
    from concourse.bass_utils import run_bass_kernel_spmd

    a = {k.replace("L0_conv_", ""): np.asarray(v) for k, v in inputs.items()}
    L = LAYERS

    def off_layout(w):
        lead = w.shape[:-4]
        w = w.reshape(*lead, TAPS, 2, w.shape[-3], TAPS)
        w = np.moveaxis(w, [-4, -3, -2, -1], [-1, -4, -3, -2])
        return np.concatenate([w, w, w, np.zeros(w.shape[:-1] + (5,), w.dtype)], axis=-1)

    def off_bias(b):
        b = b.reshape(TAPS, 2).T
        b = np.concatenate([b, b, b, np.zeros((2, 5), b.dtype)], axis=-1)
        return np.concatenate([b] * 4, axis=-1)

    dc = a["deconv_w"][:, :, :, ::-1, ::-1].reshape(L, CH, CH, TAPS).transpose(0, 1, 3, 2)
    dcn = a["dcn_w"].reshape(L, CH, CH, TAPS).transpose(0, 2, 3, 1)
    fin_off = off_layout(a["fin_off_w"])
    fin_off = fin_off.reshape(2, 2, CH, TAPS, 32).transpose(1, 0, 2, 3, 4)
    fin_dcn = a["fin_dcn_w"].reshape(CH, 2, CH, TAPS).transpose(1, 2, 3, 0)
    bias = np.zeros((L + 1, 128, 4), np.float32)
    for l in range(L + 1):
        dcn_b = a["dcn_b"][l] if l < L else a["fin_dcn_b"]
        off_b = a["off_b"][l] if l < L else a["fin_off_b"]
        if l < L:
            bias[l, :, 0] = np.concatenate([a["deconv_b"][l]] * IMG)
        bias[l, :, 1] = np.concatenate([dcn_b] * IMG)
        bias[l, :, 2:4] = off_bias(off_b).T
    sel, base, consts, ident = _tables()
    arrays = {
        "x": a["x"], "dc_w": dc, "off_w": off_layout(a["off_w"]), "dcn_w": dcn, "fin_off_w": fin_off, "fin_dcn_w": fin_dcn,
        "bias": bias, "sel": sel.reshape(128, -1).astype(ml_dtypes.bfloat16), "basec": base, "consts": consts, "ident": ident,
    }
    nc = bacc.Bacc("TRN2", target_bir_lowering=False, num_devices=1)
    feed, t = {}, {}
    for name, v in arrays.items():
        v = np.ascontiguousarray(v)
        feed[f"{name}_dram"] = v
        t[name] = nc.dram_tensor(f"{name}_dram", v.shape, mybir.dt.from_np(v.dtype), kind="ExternalInput").ap()
    t["out"] = nc.dram_tensor("out_dram", a["x"].shape, F32, kind="ExternalOutput").ap()
    build(nc, t)
    return run_bass_kernel_spmd(nc, [feed], core_ids=[0]).results[0]["out_dram"]
```

```python
import concourse.bass as bass
import numpy as np
from concourse import mybir
from contextlib import ExitStack

ACT = mybir.ActivationFunctionType
ALU = mybir.AluOpType
AX = mybir.AxisListType
F32 = mybir.dt.float32
BF16 = mybir.dt.bfloat16
I32 = mybir.dt.int32

LAYERS = 4
GROUPS = 2
IMG = 4
CH = 32
SIDE = 64
TAPS = 9
PIX = SIDE * SIDE
XP = SIDE + 2
XSIZE = XP * XP
MARGIN = 6
HP = SIDE + 2 * MARGIN
HSIZE = HP * HP
BLK = 4
BPIX = BLK * BLK
BIG = 128
NBIG = PIX // BIG
PARTS = 3
OFFS = 2 * TAPS * IMG
SPLIT_ROWS = PARTS * TAPS
ROW_ONE, ROW_PIXEL, ROW_BLOCK = SPLIT_ROWS, SPLIT_ROWS + 1, SPLIT_ROWS + 2
CONV_ROWS = 8
CONVS = SIDE // CONV_ROWS
CONV_PX = CONV_ROWS * SIDE
EPS = 1e-5
BOUND0, BOUND1 = 2.0, 5.0


class Shape:

    def __init__(self, kind, sources):
        self.kind, self.sources = kind, sources
        self.tiles = 1 if kind == 0 else 2
        self.margin = 3 if kind == 0 else MARGIN
        self.win = BLK + 2 * self.margin
        self.rows = self.win // self.tiles
        self.npos = self.rows * self.win
        self.cols = 32 if kind == 0 else 16
        self.px = BLK * self.cols
        self.chunks = PIX // self.px
        self.blocks = self.cols // BLK
        if kind == 0:
            self.groups = [4] * 9
        elif sources == 1:
            self.groups = [6] * 6
        else:
            self.groups = [8, 8, 8, 8, 4]
        self.starts = [sum(self.groups[:j]) for j in range(len(self.groups))]
        self.bank = max(self.groups) * self.px
        self.jobs = self.blocks * sources // 4
        self.parts = [(s, w) for s in range(sources) for w in range(0, self.blocks, 4)]
        order = []
        ngr = len(self.groups)
        for j in range(ngr):
            if j == ngr - 2:
                order.append(("deform", 0))
            order.append(("coord", j))
        order += [("window", j) for j in range(self.jobs)]
        self.order = order
        self.uses = len(order)
        assert self.uses % 2 == 0
        self.slot = {use: n for n, use in enumerate(order)}
        self.after = {}
        for n in range(len(self.parts)):
            self.after.setdefault(min(2 + n, ngr - 3), []).append(n)


def build(nc, t):
    ctx = ExitStack()
    with ctx:
        def sb(name, shape, dt=F32):
            return ctx.enter_context(nc.sbuf_tensor(name, shape, dt))

        def sem(name):
            return ctx.enter_context(nc.semaphore(name))

        off_store = nc.dram_tensor("off_store", (2, PARTS, TAPS, IMG, PIX), BF16)
        gn_store = nc.dram_tensor("gn_store", (GROUPS, 128, PIX), F32)

        X = sb("X", [128, GROUPS * XSIZE + 8])
        H = sb("H", [128, 2 * HSIZE + 64])
        A = sb("A", [128, 2, 36 * BIG])
        VT = sb("VT", [128, 16, 128])
        WIN = sb("WIN", [128, 4 * 256])
        AXY = sb("AXY", [128, 2, 3 * 512])
        SMP0 = sb("SMP0", [128, 8 * 144])
        DW = sb("DW", [128, TAPS * 128])
        TMP = sb("TMP", [128, BIG])
        OC = sb("OC", [128, 2, IMG * BIG], BF16)
        FOFF = sb("FOFF", [OFFS, 2, CONV_PX])
        REST = sb("REST", [OFFS, CONV_PX])
        PART = sb("PART", [OFFS, 2, PARTS, CONV_PX], BF16)
        OW = sb("OW", [128, 2, TAPS * OFFS])
        CW = sb("CW", [128, 2, TAPS * 128])
        SEL = sb("SEL", [128, 5, TAPS * 128], BF16)
        BIAS = sb("BIAS", [128, 3])
        CONST = sb("CONST", [128, 9])
        MX = sb("MX", [128, CONVS + 4])
        FLAG = sb("FLAG", [128, 1], I32)
        IDENT = sb("IDENT", [128, 128])
        SMP = [SMP0, DW]
        P = [ctx.enter_context(nc.psum_tensor(f"P{i}", [128, 3, 512], F32)) for i in range(2)]
        PS = ctx.enter_context(nc.psum_tensor("PS", [128, 2, 512], F32))

        bar = sem("bar")
        passed = sem("passed")
        loaded = sem("loaded")
        weights_loaded = sem("weights_loaded")
        x_loaded = [sem(f"x_loaded{g}") for g in range(GROUPS)]
        gn_step = sem("gn_step")
        gn_done = sem("gn_done")
        gn_root = sem("gn_root")
        gn_stored = sem("gn_stored")
        final_loaded = sem("final_loaded")
        out_stored = sem("out_stored")
        conv_full = sem("conv_full")
        conv_free = sem("conv_free")
        off_full = sem("off_full")
        off_free = sem("off_free")
        max_done = sem("max_done")
        split_step = sem("split_step")
        split_done = sem("split_done")
        parts_stored = [sem(f"parts_stored{i}") for i in range(2)]
        flag_step = sem("flag_step")
        copied = sem("copied")
        oc_full = [sem(f"oc_full{i}") for i in range(2)]
        win_full = sem("win_full")
        ring_full = sem("ring_full")
        ring_free = sem("ring_free")
        clamp_done = sem("clamp_done")
        hats_full = sem("hats_full")
        smp_full = sem("smp_full")
        smp_free = sem("smp_free")
        res_done = sem("res_done")
        turn = sem("turn")
        stepwise = [conv_full, conv_free, off_full, off_free, max_done, split_step, split_done, *parts_stored, flag_step,
                    copied,
                    *oc_full, win_full, ring_full, ring_free, clamp_done, hats_full, smp_full, smp_free, res_done, turn]
        credit = [(conv_free, 2), (off_free, 2), (max_done, 2), (split_done, 2), (ring_free, 2), (smp_full, 1),
                  (smp_free, 1), (res_done, 1), (turn, 1)]

        def x_view(group, row, col, rows, cols):
            start = group * XSIZE + row * XP + col
            return X[:, bass.ds(start, rows * XP)].rearrange("p (r c) -> p r c", c=XP)[:, :, 0:cols]

        def h_view(source, row, col, rows, cols):
            start = source * HSIZE + (row + MARGIN) * HP + col + MARGIN
            return H[:, bass.ds(start, rows * HP)].rearrange("p (r c) -> p r c", c=HP)[:, :, 0:cols]

        def out_view(group, row, col, cols):
            start = group * XSIZE + row * SIDE + col
            return X[:, bass.ds(start, BLK * SIDE)].rearrange("p (r c) -> p r c", c=SIDE)[:, :, 0:cols]

        def place(sh, c):
            per_row = SIDE // sh.cols
            return (c // per_row) * BLK, (c % per_row) * sh.cols

        def win_view(sh, slot):
            size = sh.win * sh.win
            return WIN[:, slot * (128 if sh.kind == 0 else 256):][:, 0:size]

        def smp_px(source, first_block, blocks):
            return SMP[source][:, first_block * 144:(first_block + blocks) * 144]

        def wait_alone(eng, semaphore, value):
            eng.wait_ge(semaphore, value)
            eng.sem_inc(passed, 1)

        def barrier(eng, count):
            eng.drain().then_inc(bar, 1)
            wait_alone(eng, bar, 5 * (count + 1))

        def clear_step(eng, count, clears):
            barrier(eng, count)
            if clears:
                for s in stepwise:
                    eng.sem_clear(s)
                for s, n in credit:
                    eng.sem_inc(s, n)
            barrier(eng, count + 1)

        BARS = 4

        def each_step(eng, layer_start, step, clears=False):
            clear_step(eng, 0, clears)
            with eng.Fori(0, LAYERS) as layer:
                layer_start(layer, False)
                with eng.Fori(0, GROUPS) as group:
                    step(layer, group, 2 + BARS * (layer * GROUPS + group), False)
            layer_start(LAYERS, True)
            with eng.Fori(0, GROUPS) as group:
                step(LAYERS, group, 2 + BARS * (LAYERS * GROUPS + group), True)

        def sampling(eng, bar_count, final, body, fallback, clears=False):
            barrier(eng, bar_count)
            kind = eng.value_load(FLAG[0:1, 0:1], min_val=0, max_val=2)
            sources = 2 if final else 1
            with eng.If(kind < 1):
                body(Shape(0, sources))
            with eng.If(kind == 1):
                body(Shape(1, sources))
            with eng.If(kind > 1):
                fallback(Shape(1, sources))
            barrier(eng, bar_count + 1)
            clear_step(eng, bar_count + 2, clears)

        def chunk_loop(eng, sh, body, tail):
            body(0, 0, True, False)
            with eng.Fori(0, (sh.chunks - 2) // 2) as pair:
                body(2 * pair + 1, 1, False, False)
                body(2 * pair + 2, 0, False, False)
            body(sh.chunks - 1, 1, False, True)
            tail(sh.chunks)

        def turns(sh):
            n = 2
            ngr = len(sh.groups)
            T = dict(window=0, transpose=1, keep=2)
            n = 3
            for j in range(ngr):
                T["coord", j], T["abs", j], T["clamp", j], T["product", j] = n, n + 1, n + 2, n + 3
                if j == 0:
                    pass
                n += 4
            for s in range(sh.sources):
                T["sample", s], T["read", s], T["add", s] = n, n + 1, n + 2
                n += 3
            T["n"] = n
            return T

        WINDOWS = 16

        def turn_base(T, c, p=None):
            per_chunk = WINDOWS * T["n"] + 5
            return c * per_chunk + (2 if p is None else 2 + p * T["n"]) + 1

        block = ctx.enter_context(nc.Block())

        @block.sync
        def _(sp):
            for g in range(GROUPS):
                src = t["x"][IMG * g:IMG * (g + 1)].rearrange("b c h w -> (b c) (h w)")
                sp.dma_start(A[:, g, 0:PIX], src).then_inc(x_loaded[g], 16)
            sp.dma_start(SEL[:, :, :].rearrange("p a b -> p (a b)"), t["sel"]).then_inc(loaded, 16)
            sp.dma_start(OC[:, :, :].rearrange("p a b -> p (a b)"), t["coords"]).then_inc(loaded, 16)
            sp.dma_start(CONST[:, :], t["consts"]).then_inc(loaded, 16)
            sp.dma_start(IDENT[:, :], t["ident"]).then_inc(loaded, 16)
            for g in range(GROUPS):
                sp.wait_ge(gn_done, g + 1)
                sp.dma_start(gn_store[g].rearrange("p (r c) -> p r c", c=SIDE),
                             x_view(g, 1, 1, SIDE, SIDE)).then_inc(gn_stored, 16)
            sp.wait_ge(gn_stored, 32)

            def layer_start(layer, final):
                def load(dst, src):
                    sp.dma_start(dst, src).then_inc(weights_loaded, 16)

                def pick(name):
                    return t[name][bass.ds(layer, 1)].rearrange("a p c -> (a p) c")

                load(BIAS[:, :], pick("bias"))
                if final:
                    for s in range(2):
                        load(OW[:, s, :], t["fin_off_w"][s])
                        load(CW[:, s, :], t["fin_dcn_w"][s])
                else:
                    load(DW[:, :], pick("dc_w"))
                    load(OW[:, 0, :], pick("off_w"))
                    load(CW[:, 0, :], pick("dcn_w"))

            def store_parts():
                for i in range(CONVS):
                    sp.wait_ge(split_done, i + 3)
                    for yx in range(2):
                        rows = slice(OFFS // 2 * yx, OFFS // 2 * (yx + 1))
                        dst = off_store[yx].rearrange("s k i x -> (k i) s x")[:, :, CONV_PX * i:CONV_PX * (i + 1)]
                        sp.dma_start(dst, PART[rows, i % 2, :, :]).then_inc(parts_stored[i % 2], 16)
                for par in range(2):
                    sp.wait_ge(parts_stored[par], 16 * 2 * CONVS // 2)

            def stage(sh, c, par):
                at = (c if sh.kind == 0 else c // 2) * BIG
                for yx in range(2):
                    src = off_store[yx].rearrange("s k i x -> (s k) i x")[:, :, bass.ds(at, BIG)]
                    dst = OC[CH * yx:CH * yx + SPLIT_ROWS, par, :].rearrange("p (i x) -> p i x", i=IMG)
                    sp.dma_start(dst, src).then_inc(oc_full[par], 16)

            def body_of(sh):
                coord_last = sh.slot["coord", len(sh.groups) - 1]

                def body(c, par, first, last):
                    if first:
                        stage(sh, 0, 0)
                        stage(sh, 1, 1)
                    elif not last:
                        sp.wait_ge(ring_full, (c - 1) * sh.uses + coord_last + 1)
                        stage(sh, c + 1, 1 - par)

                chunk_loop(sp, sh, body, lambda c: None)

            def fallback(sh):
                T = turns(sh)
                with sp.Fori(0, sh.chunks) as c:
                    sp.wait_ge(turn, turn_base(T, c) - 2)
                    stage(sh, c, 0)
                    for yx in range(2):
                        row = CH * yx + ROW_BLOCK
                        sp.dma_start(OC[row:row + 1, 0, :],
                                     t["blocks"][yx:yx + 1, bass.ds(c // 2 * IMG * BIG, IMG * BIG)]).then_inc(oc_full[0], 16)
                    sp.wait_ge(oc_full[0], 16 * 4 * (c + 1))
                    sp.sem_inc(turn, 1)
                wait_alone(sp, turn, turn_base(T, sh.chunks) - 2)
                sp.dma_start(OC[:, :, :].rearrange("p a b -> p (a b)"), t["coords"]).then_inc(oc_full[0], 16)
                sp.wait_ge(oc_full[0], 16 * (4 * sh.chunks + 1))

            def step(layer, group, bar_count, final):
                if final:
                    sp.dma_start(h_view(1, 0, 0, SIDE, SIDE),
                                 gn_store[bass.ds(group, 1)].rearrange("a p (r c) -> p (a r) c", c=SIDE)).then_inc(final_loaded, 16)
                    sp.wait_ge(copied, 1)
                    sp.dma_start(X[:, bass.ds(group * XSIZE, PIX)],
                                 t["x"][bass.ds(group * IMG, IMG)].rearrange("b c h w -> (b c) (h w)")).then_inc(final_loaded, 16)
                    wait_alone(sp, final_loaded, 32 * group + 32)
                store_parts()
                sampling(sp, bar_count, final, body_of, fallback)
                if final:
                    sp.dma_start(t["out"][bass.ds(group * IMG, IMG)].rearrange("b c h w -> (b c) (h w)"),
                                 X[:, bass.ds(group * XSIZE, PIX)]).then_inc(out_stored, 16)

            each_step(sp, layer_start, step)
            sp.wait_ge(out_stored, 16 * GROUPS)

        N_LOADS = 4
        N_FINAL_LOADS = 5

        def wait_weights(eng, layer, final):
            if final:
                eng.wait_ge(weights_loaded, 16 * (LAYERS * N_LOADS + N_FINAL_LOADS))
            else:
                wait_alone(eng, weights_loaded, 16 * N_LOADS * (layer + 1))

        @block.tensor
        def _(pe):
            def layer_start(layer, final):
                wait_weights(pe, layer, final)

            def first_conv(group):
                for i in range(CONVS):
                    pe.wait_ge(conv_free, i + 1)
                    for k in range(TAPS):
                        mm = nc.tensor.matmul(P[0][:, i % 2, :], DW[:, 128 * k:128 * (k + 1)],
                                              x_view(group, i * CONV_ROWS + k // 3, k % 3, CONV_ROWS, SIDE),
                                              start=k == 0, stop=k == TAPS - 1)
                    mm.then_inc(conv_full, 1)

            def offset_conv(sources):
                for i in range(CONVS):
                    pe.wait_ge(off_free, i + 1)
                    for s in range(sources):
                        for k in range(TAPS):
                            mm = nc.tensor.matmul(P[1][0:OFFS, i % 2, :], OW[:, s, OFFS * k:OFFS * (k + 1)],
                                                  h_view(s, i * CONV_ROWS + k // 3 - 1, k % 3 - 1, CONV_ROWS, SIDE),
                                                  start=s == 0 and k == 0, stop=s == sources - 1 and k == TAPS - 1)
                    mm.then_inc(off_full, 1)

            def coord(sh, j, slot, par):
                for i in range(sh.groups[j]):
                    img, tap = divmod(sh.starts[j] + i, TAPS)
                    for n in range(sh.tiles + 1):
                        yx = 1 if n == sh.tiles else 0
                        table = n if sh.kind == 0 else 2 + n
                        off = OC[:, par, BIG * img:BIG * (img + 1)]
                        if sh.kind:
                            off = off.rearrange("p (r h c) -> p h r c", r=BLK, h=2)[:, coord_half[0]]
                        mm = nc.tensor.matmul(P[slot][0:sh.npos, n, i * sh.px:(i + 1) * sh.px],
                                              SEL[:, table, 128 * tap:128 * tap + sh.npos],
                                              off, start=True, stop=True)
                return mm

            coord_half = [0]

            def sample(sh, source, first, par, tile_of):
                for w in range(4):
                    out = PS[:, w // 2, 144 * (w % 2):144 * (w % 2) + 144]
                    for n in range(sh.tiles):
                        a = A[0:sh.npos, par, n * 36 * sh.px:(n + 1) * 36 * sh.px].rearrange(
                            "p (k y x) -> p k y x", k=36, y=BLK)
                        for img in range(IMG):
                            q = slice(CH * img, CH * (img + 1))
                            mm = nc.tensor.matmul(
                                out[q].rearrange("p (k y x) -> p k y x", k=TAPS, y=BLK),
                                VT[0:sh.npos, tile_of(source, first + w, n), q],
                                a[:, TAPS * img:TAPS * (img + 1), :, BLK * (first + w):BLK * (first + w + 1)],
                                start=n == 0, stop=n == sh.tiles - 1)
                return mm

            def deform(sh, slot):
                for s in range(sh.sources):
                    for k in range(TAPS):
                        rhs = smp_px(s, 0, sh.blocks).rearrange("p (w k a) -> p w k a", k=TAPS, a=BPIX)[:, :, k, :]
                        mm = nc.tensor.matmul(P[slot][:, 0, 0:sh.px], CW[:, s, 128 * k:128 * (k + 1)], rhs,
                                              start=s == 0 and k == 0, stop=s == sh.sources - 1 and k == TAPS - 1)
                return mm

            def transpose(sh, slot, i, n, column):
                return nc.tensor.transpose(P[slot][0:sh.npos, column // 4, 128 * (column % 4):128 * (column % 4) + 128],
                                           win_view(sh, i)[:, n * sh.npos:(n + 1) * sh.npos], IDENT[:, :])

            def body_of(sh):
                tile_of = lambda s, w, n: (s * sh.blocks + w) * sh.tiles + n

                def use(c, name, j=0):
                    n = sh.slot[name, j]
                    pe.wait_ge(ring_free, c * sh.uses + n + 1)
                    return n % 2

                def part(c, n, par):
                    pe.wait_ge(hats_full, (c + 1) * len(sh.groups))
                    pe.wait_ge(smp_free, c * len(sh.parts) + n + 1)
                    sample(sh, *sh.parts[n], par, tile_of).then_inc(smp_full, 1)

                def body(c, par, first, last):
                    pe.wait_ge(oc_full[par], 16 * 2 * (c // 2 + 1))
                    coord_half[0] = par
                    for j in range(len(sh.groups)):
                        if not first and ("deform", 0) == sh.order[sh.slot["coord", j] - 1]:
                            pe.wait_ge(smp_free, c * len(sh.parts) + 1)
                            slot = use(c, "deform")
                            deform(sh, slot).then_inc(ring_full, 1)
                        elif first and ("deform", 0) == sh.order[sh.slot["coord", j] - 1]:
                            use(c, "deform")
                            pe.drain().then_inc(ring_full, 1)
                        slot = use(c, "coord", j)
                        coord(sh, j, slot, par).then_inc(ring_full, 1)
                        if not first:
                            for n in sh.after.get(j, []):
                                part(c - 1, n, 1 - par)
                    for j in range(sh.jobs):
                        pe.wait_ge(win_full, c * sh.jobs + j + 1)
                        slot = use(c, "window", j)
                        for i in range(4):
                            ws = i + (4 * (j % 2) if sh.kind == 0 else 0)
                            for n in range(sh.tiles):
                                mm = transpose(sh, slot, ws, n, i * sh.tiles + n)
                        mm.then_inc(ring_full, 1)

                def tail(c):
                    pe.wait_ge(ring_free, c * sh.uses + 2)
                    for n in range(len(sh.parts)):
                        part(c - 1, n, 1)
                    pe.wait_ge(smp_free, c * len(sh.parts) + 1)
                    deform(sh, 0).then_inc(ring_full, 1)

                chunk_loop(pe, sh, body, tail)

            def fallback(sh):
                T = turns(sh)

                def chunk(c, par):
                    coord_half[0] = par
                    with pe.Fori(0, WINDOWS) as p:
                        base = turn_base(T, c, p)
                        pe.wait_ge(turn, base + T["transpose"])
                        for s in range(sh.sources):
                            for n in range(sh.tiles):
                                mm = transpose(sh, 0, s, n, s * sh.tiles + n)
                        mm.then_inc(turn, 1)
                        for j in range(len(sh.groups)):
                            pe.wait_ge(turn, base + T["coord", j])
                            coord(sh, j, 0, 0).then_inc(turn, 1)
                        for s in range(sh.sources):
                            pe.wait_ge(turn, base + T["sample", s])
                            sample(sh, s, 0, 0, lambda s, w, n: s * sh.tiles + n).then_inc(turn, 1)
                    pe.wait_ge(turn, turn_base(T, c, WINDOWS))
                    deform_sum(sh).then_inc(turn, 1)

                def deform_sum(sh):
                    for s in range(sh.sources):
                        for k in range(TAPS):
                            rhs = smp_px(s, 4, 4).rearrange("p (w k a) -> p w k a", k=TAPS, a=BPIX)[:, :, k, :]
                            mm = nc.tensor.matmul(P[0][:, 0, 0:sh.px], CW[:, s, 128 * k:128 * (k + 1)], rhs,
                                                  start=s == 0 and k == 0, stop=s == sh.sources - 1 and k == TAPS - 1)
                    return mm

                with pe.Fori(0, sh.chunks // 2) as pair:
                    chunk(2 * pair, 0)
                    chunk(2 * pair + 1, 1)

            def step(layer, group, bar_count, final):
                if not final:
                    first_conv(group)
                    pe.wait_ge(conv_free, CONVS + 2)
                else:
                    pe.wait_ge(copied, 1)
                    wait_alone(pe, final_loaded, 32 * group + 32)
                offset_conv(2 if final else 1)
                sampling(pe, bar_count, final, body_of, fallback)

            each_step(pe, layer_start, step)

        @block.scalar
        def _(act):
            for g in range(GROUPS):
                act.wait_ge(gn_step, 1 + 4 * g + 3)
                nc.scalar.activation(MX[:, 4 * g + 2:4 * g + 3], MX[:, 4 * g + 1:4 * g + 2], ACT.Sqrt).then_inc(gn_root, 1)

            def layer_start(layer, final):
                wait_weights(act, layer, final)

            def raster(sh, slot):
                return P[slot][:, 0, 0:sh.px].rearrange("p (w y x) -> p y w x", w=sh.blocks, y=BLK)

            def tmp_view(sh):
                return TMP[:, 0:sh.px].rearrange("p (y w x) -> p y w x", y=BLK, w=sh.blocks)

            def body_of(sh, final):
                ngr = len(sh.groups)

                def out_act(c, slot):
                    act.wait_ge(res_done, c + 1)
                    nc.scalar.activation(tmp_view(sh), raster(sh, slot), ACT.Identity if final else ACT.Relu,
                                         bias=BIAS[:, 1:2]).then_inc(ring_free, 1)

                def read_part(c, n):
                    s, w = sh.parts[n]
                    act.wait_ge(smp_full, c * len(sh.parts) + n + 2)
                    nc.scalar.activation(smp_px(s, w, 4).rearrange("p (a b) -> p a b", a=2), PS[:, :, 0:288],
                                         ACT.Copy).then_inc(smp_free, 1)

                def body(c, par, first, last):
                    for j in range(ngr):
                        if ("deform", 0) == sh.order[sh.slot["coord", j] - 1]:
                            n = sh.slot["deform", 0]
                            act.wait_ge(ring_full, c * sh.uses + n + 1)
                            if first:
                                act.drain().then_inc(ring_free, 1)
                            else:
                                out_act(c - 1, n % 2)
                        n = sh.slot["coord", j]
                        act.wait_ge(ring_full, c * sh.uses + n + 1)
                        if not (first and j < 2):
                            act.wait_ge(hats_full, c * ngr + j - 1)
                        size = sh.groups[j] * sh.px
                        buf = AXY[0:sh.npos, (par * ngr + j) % 2, 0:(sh.tiles + 1) * sh.bank].rearrange(
                            "p (n a) -> p n a", n=sh.tiles + 1)
                        nc.scalar.activation(buf[:, :, 0:size], P[n % 2][0:sh.npos, 0:sh.tiles + 1, 0:size],
                                             ACT.Abs).then_inc(ring_free, 1)
                        if not first:
                            for part in sh.after.get(j, []):
                                read_part(c - 1, part)
                    for j in range(sh.jobs):
                        n = sh.slot["window", j]
                        act.wait_ge(ring_full, c * sh.uses + n + 1)
                        count = 4 * sh.tiles
                        vt = VT[0:sh.npos, j * count:(j + 1) * count, :]
                        src = P[n % 2][0:sh.npos, 0:sh.tiles, :].rearrange("p a (b c) -> p (a b) c", c=128)
                        nc.scalar.activation(vt, src, ACT.Copy).then_inc(ring_free, 1)

                def tail(c):
                    for n in range(len(sh.parts)):
                        read_part(c - 1, n)
                    act.wait_ge(ring_full, c * sh.uses + 1)
                    out_act(c - 1, 0)

                chunk_loop(act, sh, body, tail)

            def fallback_of(sh, final):
                T = turns(sh)
                with act.Fori(0, sh.chunks) as c:
                    with act.Fori(0, WINDOWS) as p:
                        base = turn_base(T, c, p)
                        wait_alone(act, turn, base + T["keep"])
                        count = sh.sources * sh.tiles
                        nc.scalar.activation(VT[:, 0:count, :], P[0][:, 0, 0:128 * count].rearrange(
                            "p (a b) -> p a b", b=128), ACT.Copy).then_inc(turn, 1)
                        for j in range(len(sh.groups)):
                            wait_alone(act, turn, base + T["abs", j])
                            size = sh.groups[j] * sh.px
                            buf = AXY[:, 0, 0:3 * sh.bank].rearrange("p (n a) -> p n a", n=3)
                            nc.scalar.activation(buf[:, 0:2, 0:size], P[0][:, 0:2, 0:size], ACT.Abs,
                                                 bias=CONST[:, bass.ds(LAYERS + 1 + p // 4, 1)])
                            nc.scalar.activation(buf[:, 2, 0:size], P[0][:, 2, 0:size], ACT.Abs,
                                                 bias=CONST[:, bass.ds(LAYERS + 1 + p % 4, 1)]).then_inc(turn, 1)
                        for s in range(sh.sources):
                            wait_alone(act, turn, base + T["read", s])
                            nc.scalar.activation(smp_px(s, 0, 4).rearrange("p (a b) -> p a b", a=2), PS[:, :, 0:288],
                                                 ACT.Copy).then_inc(turn, 1)
                    wait_alone(act, turn, turn_base(T, c, WINDOWS) + 1)
                    nc.scalar.activation(tmp_view(sh), raster(sh, 0), ACT.Identity if final else ACT.Relu,
                                         bias=BIAS[:, 1:2]).then_inc(turn, 1)

            def step(layer, group, bar_count, final):
                if not final:
                    for i in range(CONVS):
                        act.wait_ge(conv_full, i + 1)
                        nc.scalar.activation(h_view(0, i * CONV_ROWS, 0, CONV_ROWS, SIDE),
                                             P[0][:, i % 2, :].rearrange("p (r c) -> p r c", c=SIDE), ACT.Relu,
                                             bias=BIAS[:, 0:1]).then_inc(conv_free, 1)
                sampling(act, bar_count, final, lambda sh: body_of(sh, final), lambda sh: fallback_of(sh, final))

            each_step(act, layer_start, step)

        @block.vector
        def _(dve):
            nc.vector.memset(X[:, :], 0.0).then_inc(gn_step, 1)
            stats = AXY[:, 0, 0:48].rearrange("p (a b) -> p a b", b=6)
            for g in range(GROUPS):
                done = 1 + 4 * g
                dve.wait_ge(x_loaded[g], 16)
                dve.wait_ge(gn_step, done)
                for i in range(8):
                    last = nc.vector.bn_stats(stats[:, i, :], A[:, g, 512 * i:512 * (i + 1)])
                last.then_inc(gn_step, 1)
                dve.wait_ge(gn_step, done + 1)
                nc.vector.bn_aggr(MX[:, 4 * g:4 * g + 2], stats).then_inc(gn_step, 1)
                dve.wait_ge(gn_step, done + 2)
                nc.vector.tensor_scalar_add(MX[:, 4 * g + 1:4 * g + 2], MX[:, 4 * g + 1:4 * g + 2], EPS).then_inc(gn_step, 1)
                dve.wait_ge(gn_root, g + 1)
                nc.vector.reciprocal(MX[:, 4 * g + 3:4 * g + 4], MX[:, 4 * g + 2:4 * g + 3]).then_inc(gn_step, 1)
                dve.wait_ge(gn_step, done + 4)
                nc.vector.tensor_scalar(x_view(g, 1, 1, SIDE, SIDE), A[:, g, 0:PIX].rearrange("p (r c) -> p r c", c=SIDE),
                                        MX[:, 4 * g:4 * g + 1], MX[:, 4 * g + 3:4 * g + 4], ALU.subtract,
                                        ALU.mult).then_inc(gn_done, 1)
            dve.wait_ge(loaded, 64)

            def layer_start(layer, final):
                wait_weights(dve, layer, final)

            def residual(sh, layer, group, c, final):
                row, col = place(sh, c)
                tmp = TMP[:, 0:sh.px].rearrange("p (r c) -> p r c", r=BLK)
                if final:
                    dst = out_view(group, row, col, sh.cols)
                    flag = CONST[:, LAYERS:LAYERS + 1]
                else:
                    dst = x_view(group, row + 1, col + 1, BLK, sh.cols)
                    flag = CONST[:, bass.ds(layer, 1)]
                return nc.vector.scalar_tensor_tensor(dst, dst, flag, tmp, ALU.mult, ALU.add)

            def product(sh, j, buf, par):
                size = sh.groups[j] * sh.px
                a = A[0:sh.npos, par, 0:sh.tiles * 36 * sh.px].rearrange("p (n a) -> p n a", n=sh.tiles)
                a = a[:, :, sh.starts[j] * sh.px:sh.starts[j] * sh.px + size]
                hx = buf[:, sh.tiles:sh.tiles + 1, 0:size]
                if sh.tiles > 1:
                    hx = hx.broadcast_to([sh.npos, sh.tiles, size])
                return nc.vector.tensor_tensor(a, buf[:, 0:sh.tiles, 0:size], hx, ALU.mult)

            def body_of(sh, layer, group, final):
                ngr = len(sh.groups)

                def body(c, par, first, last):
                    for j in range(ngr):
                        size = sh.groups[j] * sh.px
                        n = sh.slot["coord", j]
                        if not first and ("deform", 0) == sh.order[n - 1]:
                            dve.wait_ge(ring_free, c * sh.uses + n - 1 + 3)
                            residual(sh, layer, group, c - 1, final).then_inc(res_done, 1)
                        buf = AXY[0:sh.npos, (par * ngr + j) % 2, 0:(sh.tiles + 1) * sh.bank].rearrange(
                            "p (n a) -> p n a", n=sh.tiles + 1)
                        dve.wait_ge(ring_free, c * sh.uses + n + 3)
                        nc.vector.tensor_scalar(buf[:, :, 0:size], buf[:, :, 0:size], 1.0, 1.0, ALU.min,
                                                ALU.subtract).then_inc(clamp_done, 1)
                        dve.wait_ge(clamp_done, c * ngr + j + 1)
                        if not first and j == 0:
                            dve.wait_ge(smp_full, (c - 1) * len(sh.parts) + 1)
                        product(sh, j, buf, par).then_inc(hats_full, 1)

                def tail(c):
                    dve.wait_ge(ring_free, c * sh.uses + 3)
                    residual(sh, layer, group, c - 1, final).then_inc(res_done, 1)

                chunk_loop(dve, sh, body, tail)

            def fallback_of(sh, layer, group, final):
                T = turns(sh)
                with dve.Fori(0, sh.chunks) as c:
                    dve.wait_ge(turn, turn_base(T, c) - 1)
                    for s in range(sh.sources):
                        mm = nc.vector.memset(smp_px(s, 4, 4), 0.0)
                    mm.then_inc(turn, 1)
                    with dve.Fori(0, WINDOWS) as p:
                        base = turn_base(T, c, p)
                        for j in range(len(sh.groups)):
                            size = sh.groups[j] * sh.px
                            buf = AXY[:, 0, 0:3 * sh.bank].rearrange("p (n a) -> p n a", n=3)
                            dve.wait_ge(turn, base + T["clamp", j])
                            nc.vector.tensor_scalar(buf[:, :, 0:size], buf[:, :, 0:size], 1.0, 1.0, ALU.min,
                                                    ALU.subtract).then_inc(turn, 1)
                            dve.wait_ge(turn, base + T["product", j])
                            product(sh, j, buf, 0).then_inc(turn, 1)
                        for s in range(sh.sources):
                            dve.wait_ge(turn, base + T["add", s])
                            nc.vector.tensor_tensor(smp_px(s, 4, 4), smp_px(s, 4, 4), smp_px(s, 0, 4),
                                                    ALU.add).then_inc(turn, 1)
                    dve.wait_ge(turn, turn_base(T, c, WINDOWS) + 2)
                    residual(sh, layer, group, c, final).then_inc(turn, 1)

            def step(layer, group, bar_count, final):
                if final:
                    nc.vector.tensor_copy(h_view(0, 0, 0, SIDE, SIDE), x_view(group, 1, 1, SIDE, SIDE)).then_inc(copied, 1)
                nc.vector.memset(MX[:, :], 0.0).then_inc(flag_step, 1)
                dve.wait_ge(flag_step, 1)
                for i in range(CONVS):
                    dve.wait_ge(off_full, i + 1)
                    dve.wait_ge(split_done, i + 1)
                    dve.wait_ge(max_done, i + 1)
                    for strip in range(CONV_ROWS // BLK):
                        src = P[1][0:OFFS, i % 2, 2 * BIG * strip:2 * BIG * (strip + 1)]
                        dst = FOFF[:, i % 2, 2 * BIG * strip:2 * BIG * (strip + 1)]
                        fo = nc.vector.tensor_scalar(dst.rearrange("p (h r c) -> p r h c", h=2, r=BLK),
                                                     src.rearrange("p (r h c) -> p r h c", h=2, r=BLK),
                                                     BIAS[0:OFFS, 2:3], None, ALU.add)
                    fo.then_inc(off_free, 1)
                    dve.wait_ge(off_free, i + 3)
                    nc.vector.tensor_reduce(MX[0:OFFS, i:i + 1], FOFF[:, i % 2, :], AX.X, ALU.max,
                                            apply_absolute_value=True).then_inc(max_done, 1)
                dve.wait_ge(max_done, CONVS + 2)
                nc.vector.tensor_reduce(MX[:, CONVS:CONVS + 1], MX[:, 0:CONVS], AX.X, ALU.max).then_inc(flag_step, 1)
                dve.wait_ge(flag_step, 3)
                nc.vector.tensor_scalar(MX[:, CONVS + 2:CONVS + 3], MX[:, CONVS + 1:CONVS + 2], BOUND0, None, ALU.is_ge).then_inc(flag_step, 1)
                nc.vector.tensor_scalar(MX[:, CONVS + 3:CONVS + 4], MX[:, CONVS + 1:CONVS + 2], BOUND1, None, ALU.is_ge).then_inc(flag_step, 1)
                dve.wait_ge(flag_step, 5)
                nc.vector.tensor_tensor(FLAG[:, :], MX[:, CONVS + 2:CONVS + 3], MX[:, CONVS + 3:CONVS + 4], ALU.add).then_inc(flag_step, 1)
                sampling(dve, bar_count, final, lambda sh: body_of(sh, layer, group, final),
                         lambda sh: fallback_of(sh, layer, group, final))

            each_step(dve, layer_start, step)

        @block.gpsimd
        def _(pool):
            nc.gpsimd.memset(H[:, :], 0.0)

            def body_of(sh):
                def body(c, par, first, last):
                    row, col = place(sh, c)
                    for j in range(sh.jobs):
                        back = 2 if sh.kind == 0 else 1
                        if j >= back:
                            pool.wait_ge(ring_full, c * sh.uses + sh.slot["window", j - back] + 1)
                        elif not first:
                            pool.wait_ge(ring_full, (c - 1) * sh.uses + sh.slot["window", sh.jobs + j - back] + 1)
                        for i in range(4):
                            s, w = divmod(4 * j + i, sh.blocks)
                            ws = i + (4 * (j % 2) if sh.kind == 0 else 0)
                            cp = nc.gpsimd.tensor_copy(
                                win_view(sh, ws).rearrange("p (r c) -> p r c", c=sh.win),
                                h_view(s, row - sh.margin, col + BLK * w - sh.margin, sh.win, sh.win))
                        cp.then_inc(win_full, 1)

                chunk_loop(pool, sh, body, lambda c: None)

            def fallback(sh):
                T = turns(sh)
                with pool.Fori(0, sh.chunks) as c:
                    with pool.Fori(0, WINDOWS) as p:
                        pool.wait_ge(turn, turn_base(T, c, p) + T["window"])
                        for s in range(sh.sources):
                            cp = nc.gpsimd.tensor_copy(win_view(sh, s).rearrange("p (r c) -> p r c", c=sh.win),
                                                       h_view(s, (p // 4) * 16, (p % 4) * 16, sh.win, sh.win))
                        cp.then_inc(turn, 1)

            def step(layer, group, bar_count, final):
                for i in range(CONVS):
                    foff, part = FOFF[:, i % 2, :], PART[:, i % 2]
                    pool.wait_ge(off_free, i + 3)
                    if i >= 2:
                        pool.wait_ge(parts_stored[i % 2], 16 * 2 * (i // 2))
                    nc.gpsimd.tensor_copy(part[:, 0, :], foff).then_inc(split_step, 1)
                    pool.wait_ge(split_step, 3 * i + 1)
                    nc.gpsimd.tensor_tensor(REST[:, :], foff, part[:, 0, :], ALU.subtract).then_inc(split_step, 1)
                    pool.wait_ge(split_step, 3 * i + 2)
                    nc.gpsimd.tensor_copy(part[:, 1, :], REST[:, :]).then_inc(split_step, 1)
                    pool.wait_ge(split_step, 3 * i + 3)
                    nc.gpsimd.tensor_tensor(part[:, 2, :], REST[:, :], part[:, 1, :], ALU.subtract).then_inc(split_done, 1)
                    pool.wait_ge(split_done, i + 3)
                pool.wait_ge(flag_step, 2)
                nc.gpsimd.partition_all_reduce(MX[:, CONVS + 1:CONVS + 2], MX[:, CONVS:CONVS + 1], 128,
                                               bass.bass_isa.ReduceOp.max).then_inc(flag_step, 1)
                sampling(pool, bar_count, final, body_of, fallback, clears=True)

            each_step(pool, lambda layer, final: None, step, clears=True)


def _tables():
    npos = {0: 100, 1: 128}
    sel = np.zeros((128, 5, TAPS, 128), np.float32)
    tables = [(0, 0, 0), (0, 1, 0), (1, 0, 0), (1, 0, 1), (1, 1, 0)]
    for n, (kind, yx, tile) in enumerate(tables):
        win, rows, margin = (10, 10, 3) if kind == 0 else (16, 8, 6)
        q = CH * yx
        for k in range(TAPS):
            for s in range(PARTS):
                sel[q + s * TAPS + k, n, k, :] = 1.0
            pos = np.arange(npos[kind])
            at = pos % win if yx else pos // win + rows * tile
            shift = (k % 3 if yx else k // 3) - 1
            sel[q + ROW_ONE, n, k, :npos[kind]] = shift + margin - at
            sel[q + ROW_PIXEL, n, k, :] = 1.0
            sel[q + ROW_BLOCK, n, k, :] = 1.0
    pixels = np.arange(BIG)
    coords = np.zeros((128, 2, IMG, BIG), np.float32)
    for yx in range(2):
        coords[CH * yx + ROW_ONE] = 1.0
        coords[CH * yx + ROW_PIXEL] = pixels % BLK if yx else pixels // 32
    blocks = np.zeros((2, NBIG, IMG, BIG), np.float32)
    for c in range(NBIG):
        blocks[0, c] = c // 2 * BLK
        blocks[1, c] = c % 2 * 32 + pixels % 32 // BLK * BLK
    consts = np.zeros((128, 9), np.float32)
    consts[:, 0:5] = [0.0, 1.0, 1.0, 0.0, 1.0]
    consts[:, 5:9] = -6.0 - 16.0 * np.arange(4)
    return dict(sel=sel.reshape(128, -1), coords=coords.reshape(128, -1), blocks=blocks.reshape(2, -1)), consts


def kernel(**inputs):
    import concourse.bacc as bacc
    import ml_dtypes
    from concourse.bass_utils import run_bass_kernel_spmd

    a = {k.replace("L0_conv_", ""): np.asarray(v) for k, v in inputs.items()}
    L = LAYERS

    def diagonal(w):
        full = np.zeros((IMG, CH, TAPS, IMG, CH), w.dtype)
        for i in range(IMG):
            full[i, :, :, i] = w
        return full.reshape(128, TAPS * 128)

    def diagonal_off(w):
        w = w.reshape(TAPS, 2, CH, TAPS)
        full = np.zeros((IMG, CH, TAPS, 2, TAPS, IMG), w.dtype)
        for i in range(IMG):
            full[i, :, :, :, :, i] = w.transpose(2, 3, 1, 0)
        return full.reshape(128, TAPS * OFFS)

    dc = np.stack([diagonal(w[:, :, ::-1, ::-1].reshape(CH, CH, TAPS).transpose(0, 2, 1)) for w in a["deconv_w"]])
    dcn = np.stack([diagonal(w.reshape(CH, CH, TAPS).transpose(1, 2, 0)) for w in a["dcn_w"]])
    off = np.stack([diagonal_off(w.reshape(2 * TAPS, CH, TAPS)) for w in a["off_w"]])
    fin_off, fin_dcn = a["fin_off_w"], a["fin_dcn_w"]
    fin_off = np.stack([diagonal_off(fin_off[:, CH * s:CH * (s + 1)].reshape(2 * TAPS, CH, TAPS)) for s in range(2)])
    fin_dcn = np.stack([diagonal(fin_dcn[:, CH * s:CH * (s + 1)].reshape(CH, CH, TAPS).transpose(1, 2, 0))
                        for s in range(2)])
    bias = np.zeros((L + 1, 128, 3), np.float32)
    for l in range(L + 1):
        dcn_b = a["dcn_b"][l] if l < L else a["fin_dcn_b"]
        off_b = a["off_b"][l] if l < L else a["fin_off_b"]
        if l < L:
            bias[l, :, 0] = np.tile(a["deconv_b"][l], IMG)
        bias[l, :, 1] = np.tile(dcn_b, IMG)
        bias[l, :OFFS, 2] = np.repeat(off_b.reshape(TAPS, 2).T.reshape(-1), IMG)
    tables, consts = _tables()
    arrays = {"x": a["x"], "dc_w": dc, "off_w": off, "dcn_w": dcn, "fin_off_w": fin_off, "fin_dcn_w": fin_dcn, "bias": bias,
              "consts": consts, "ident": np.eye(128, dtype=np.float32)}
    for name, table in tables.items():
        arrays[name] = table.astype(ml_dtypes.bfloat16)
    nc = bacc.Bacc("TRN2", target_bir_lowering=False, num_devices=1)
    feed, t = {}, {}
    for name, v in arrays.items():
        v = np.ascontiguousarray(v)
        feed[f"{name}_dram"] = v
        t[name] = nc.dram_tensor(f"{name}_dram", v.shape, mybir.dt.from_np(v.dtype), kind="ExternalInput").ap()
    t["out"] = nc.dram_tensor("out_dram", a["x"].shape, F32, kind="ExternalOutput").ap()
    build(nc, t)
    return run_bass_kernel_spmd(nc, [feed], core_ids=[0]).results[0]["out_dram"]
```

```python
import concourse.bass as bass
import numpy as np
from concourse import mybir
from contextlib import ExitStack

ACT = mybir.ActivationFunctionType
ALU = mybir.AluOpType
AX = mybir.AxisListType
F32 = mybir.dt.float32
BF16 = mybir.dt.bfloat16
I32 = mybir.dt.int32

LAYERS = 4
GROUPS = 2
IMG = 4
CH = 32
SIDE = 64
TAPS = 9
PIX = SIDE * SIDE
XP = SIDE + 2
XSIZE = XP * XP
MARGIN = 6
HP = SIDE + 2 * MARGIN
HSIZE = HP * HP
BLK = 4
BPIX = BLK * BLK
BIG = 128
NBIG = PIX // BIG
PARTS = 3
OFFS = 2 * TAPS * IMG
SPLIT_ROWS = PARTS * TAPS
ROW_ONE, ROW_PIXEL, ROW_BLOCK = SPLIT_ROWS, SPLIT_ROWS + 1, SPLIT_ROWS + 2
CONV_ROWS = 8
CONVS = SIDE // CONV_ROWS
CONV_PX = CONV_ROWS * SIDE
EPS = 1e-5
BOUND0, BOUND1 = 2.0, 5.0
AXY_BUFS = 3
RING = 3


class Shape:

    def __init__(self, kind, sources):
        self.kind, self.sources = kind, sources
        self.tiles = 1 if kind == 0 else 2
        self.margin = 3 if kind == 0 else MARGIN
        self.win = BLK + 2 * self.margin
        self.rows = self.win // self.tiles
        self.npos = self.rows * self.win
        self.cols = 32 if kind == 0 else 16
        self.px = BLK * self.cols
        self.chunks = PIX // self.px
        self.blocks = self.cols // BLK
        self.groups = [6] * 6 if kind and sources == 1 else [4] * 9
        self.starts = [sum(self.groups[:j]) for j in range(len(self.groups))]
        self.bank = max(self.groups) * self.px
        self.jobs = self.blocks * sources // 4
        self.parts = [(s, w) for s in range(sources) for w in range(0, self.blocks, 2)]
        ngr = len(self.groups)
        spots, window_spot = ([2, 3, 4, 5], 7) if kind == 0 else ([2, 3], 4) if sources == 1 else ([2, 3, 4, 6], 3)
        per_spot = (len(self.parts) + len(spots) - 1) // len(spots)
        self.after = {}
        for n in range(len(self.parts)):
            self.after.setdefault(spots[n // per_spot], []).append(n)
        cuts = {1: [2, 2], 2: [4, 2, 2], 4: [4, 4, 2, 2, 2, 2]}[self.jobs]
        self.windows = [(sum(cuts[:i]), cuts[i]) for i in range(len(cuts))]
        order = [("coord", j) for j in range(ngr)]
        order.insert(window_spot + 1, ("window", 0))
        order += [("window", i) for i in range(1, len(self.windows))]
        self.thirds = [("window", 0), ("coord", ngr - 1), ("window", 1)] if window_spot == ngr - 2 else [
            ("coord", ngr - 1), ("window", 1), ("window", 2)]
        self.ps_uses = len(self.parts) + 1
        self.order = order
        self.uses = len(order)
        self.slot = {use: n for n, use in enumerate(order)}
        self.job_last = [self.slot["window", [first + count for first, count in self.windows].index(4 * job + 4)]
                         for job in range(self.jobs)]
        self.banks = self.tiles + 1
        self.depth = 3 if kind == 0 and self.uses % 3 == 0 else 2
        assert self.uses % self.depth == 0 and ngr % AXY_BUFS == 0 and len(self.parts) % 2 == 0


def build(nc, t):
    ctx = ExitStack()
    with ctx:
        def sb(name, shape, dt=F32):
            return ctx.enter_context(nc.sbuf_tensor(name, shape, dt))

        def sem(name):
            return ctx.enter_context(nc.semaphore(name))

        off_store = nc.dram_tensor("off_store", (2, PARTS, TAPS, IMG, PIX), BF16)
        gn_store = nc.dram_tensor("gn_store", (GROUPS, 128, PIX), F32)

        X = sb("X", [128, GROUPS * XSIZE + 8])
        H = sb("H", [128, 2 * HSIZE + 64])
        A = sb("A", [128, 2, 36 * BIG])
        VT = sb("VT", [128, 16, 128])
        WIN = sb("WIN", [128, 8 * 256])
        AXY = sb("AXY", [128, AXY_BUFS, 3 * 384])
        SMP0 = sb("SMP0", [128, 8 * 144])
        DW = sb("DW", [128, TAPS * 128])
        TMP = sb("TMP", [128, BIG])
        OC = sb("OC", [128, 2, IMG * BIG], BF16)
        FOFF = sb("FOFF", [OFFS, 2, CONV_PX])
        REST = sb("REST", [OFFS, CONV_PX])
        PART = sb("PART", [OFFS, 2, PARTS, CONV_PX], BF16)
        OW = sb("OW", [128, 2, TAPS * OFFS])
        CW = sb("CW", [128, 2, TAPS * 128])
        SEL = sb("SEL", [128, 5, TAPS * 128], BF16)
        BIAS = sb("BIAS", [128, 3])
        CONST = sb("CONST", [128, 9])
        MX = sb("MX", [128, CONVS + 4])
        FLAG = sb("FLAG", [128, 1], I32)
        IDENT = sb("IDENT", [128, 128])
        SMP = [SMP0, DW]
        P = ctx.enter_context(nc.psum_tensor("P", [128, 6, 512], F32))
        PS = ctx.enter_context(nc.psum_tensor("PS", [128, 2, 512], F32))

        bar = sem("bar")
        passed = sem("passed")
        loaded = sem("loaded")
        weights_loaded = sem("weights_loaded")
        x_loaded = [sem(f"x_loaded{g}") for g in range(GROUPS)]
        gn_step = sem("gn_step")
        gn_done = sem("gn_done")
        gn_root = sem("gn_root")
        gn_stored = sem("gn_stored")
        final_loaded = sem("final_loaded")
        out_stored = sem("out_stored")
        conv_full = sem("conv_full")
        conv_free = sem("conv_free")
        off_full = sem("off_full")
        off_free = sem("off_free")
        max_done = sem("max_done")
        split_step = sem("split_step")
        split_done = sem("split_done")
        parts_stored = [sem(f"parts_stored{i}") for i in range(2)]
        flag_step = sem("flag_step")
        copied = sem("copied")
        oc_full = [sem(f"oc_full{i}") for i in range(2)]
        win_full = sem("win_full")
        ring_full = sem("ring_full")
        ring_free = sem("ring_free")
        clamp_done = sem("clamp_done")
        hats_full = sem("hats_full")
        smp_full = sem("smp_full")
        smp_free = sem("smp_free")
        res_done = sem("res_done")
        turn = sem("turn")
        stepwise = [conv_full, conv_free, off_full, off_free, max_done, split_step, split_done, *parts_stored, flag_step,
                    copied,
                    *oc_full, win_full, ring_full, ring_free, clamp_done, hats_full, smp_full, smp_free, res_done, turn]
        credit = [(conv_free, 2), (off_free, 2), (max_done, 2), (split_done, 2), (ring_free, RING), (smp_full, 2),
                  (smp_free, 2), (res_done, 1), (turn, 1)]

        def x_view(group, row, col, rows, cols):
            start = group * XSIZE + row * XP + col
            return X[:, bass.ds(start, rows * XP)].rearrange("p (r c) -> p r c", c=XP)[:, :, 0:cols]

        def h_view(source, row, col, rows, cols):
            start = source * HSIZE + (row + MARGIN) * HP + col + MARGIN
            return H[:, bass.ds(start, rows * HP)].rearrange("p (r c) -> p r c", c=HP)[:, :, 0:cols]

        def out_view(group, row, col, cols):
            start = group * XSIZE + row * SIDE + col
            return X[:, bass.ds(start, BLK * SIDE)].rearrange("p (r c) -> p r c", c=SIDE)[:, :, 0:cols]

        def place(sh, c):
            per_row = SIDE // sh.cols
            return (c // per_row) * BLK, (c % per_row) * sh.cols

        def win_view(sh, slot):
            size = sh.win * sh.win
            return WIN[:, slot * 256:slot * 256 + size]

        def bank(sh, slot, n):
            return P[:, slot * sh.banks + n, :]

        def distances(sh, j):
            return AXY[0:sh.npos, j % AXY_BUFS, 0:sh.banks * sh.bank].rearrange("p (n a) -> p n a", n=sh.banks)

        def smp_px(source, first_block, blocks):
            return SMP[source][:, first_block * 144:(first_block + blocks) * 144]

        def wait_alone(eng, semaphore, value):
            eng.wait_ge(semaphore, value)
            eng.sem_inc(passed, 1)

        def barrier(eng, count):
            eng.drain().then_inc(bar, 1)
            wait_alone(eng, bar, 5 * (count + 1))

        def clear_step(eng, count, clears):
            barrier(eng, count)
            if clears:
                for s in stepwise:
                    eng.sem_clear(s)
                for s, n in credit:
                    eng.sem_inc(s, n)
            barrier(eng, count + 1)

        BARS = 4

        def each_step(eng, layer_start, step, clears=False):
            clear_step(eng, 0, clears)
            with eng.Fori(0, LAYERS) as layer:
                layer_start(layer, False)
                with eng.Fori(0, GROUPS) as group:
                    step(layer, group, 2 + BARS * (layer * GROUPS + group), False)
            layer_start(LAYERS, True)
            with eng.Fori(0, GROUPS) as group:
                step(LAYERS, group, 2 + BARS * (LAYERS * GROUPS + group), True)

        def sampling(eng, bar_count, final, body, fallback, clears=False):
            barrier(eng, bar_count)
            kind = eng.value_load(FLAG[0:1, 0:1], min_val=0, max_val=2)
            sources = 2 if final else 1
            with eng.If(kind < 1):
                body(Shape(0, sources))
            with eng.If(kind == 1):
                body(Shape(1, sources))
            with eng.If(kind > 1):
                fallback(Shape(1, sources))
            barrier(eng, bar_count + 1)
            clear_step(eng, bar_count + 2, clears)

        def chunk_loop(eng, sh, body, tail):
            body(0, 0, True, False)
            with eng.Fori(0, (sh.chunks - 2) // 2) as pair:
                body(2 * pair + 1, 1, False, False)
                body(2 * pair + 2, 0, False, False)
            body(sh.chunks - 1, 1, False, True)
            tail(sh.chunks)

        def turns(sh):
            T = dict(window=0, transpose=1, keep=2)
            n = 3
            for j in range(len(sh.groups)):
                T["coord", j], T["abs", j], T["clamp", j], T["product", j] = n, n + 1, n + 2, n + 3
                n += 4
            for s in range(sh.sources):
                T["sample", s], T["read", s], T["add", s] = n, n + 1, n + 2
                n += 3
            T["n"] = n
            return T

        WINDOWS = 16

        def turn_base(T, c, p=None):
            per_chunk = WINDOWS * T["n"] + 5
            return c * per_chunk + (2 if p is None else 2 + p * T["n"]) + 1

        block = ctx.enter_context(nc.Block())

        @block.sync
        def _(sp):
            for g in range(GROUPS):
                src = t["x"][IMG * g:IMG * (g + 1)].rearrange("b c h w -> (b c) (h w)")
                sp.dma_start(A[:, g, 0:PIX], src).then_inc(x_loaded[g], 16)
            sp.dma_start(SEL[:, :, :].rearrange("p a b -> p (a b)"), t["sel"]).then_inc(loaded, 16)
            sp.dma_start(OC[:, :, :].rearrange("p a b -> p (a b)"), t["coords"]).then_inc(loaded, 16)
            sp.dma_start(CONST[:, :], t["consts"]).then_inc(loaded, 16)
            sp.dma_start(IDENT[:, :], t["ident"]).then_inc(loaded, 16)
            for g in range(GROUPS):
                sp.wait_ge(gn_done, g + 1)
                sp.dma_start(gn_store[g].rearrange("p (r c) -> p r c", c=SIDE),
                             x_view(g, 1, 1, SIDE, SIDE)).then_inc(gn_stored, 16)
            sp.wait_ge(gn_stored, 32)

            def layer_start(layer, final):
                def load(dst, src):
                    sp.dma_start(dst, src).then_inc(weights_loaded, 16)

                def pick(name):
                    return t[name][bass.ds(layer, 1)].rearrange("a p c -> (a p) c")

                load(BIAS[:, :], pick("bias"))
                if final:
                    for s in range(2):
                        load(OW[:, s, :], t["fin_off_w"][s])
                        load(CW[:, s, :], t["fin_dcn_w"][s])
                else:
                    load(DW[:, :], pick("dc_w"))
                    load(OW[:, 0, :], pick("off_w"))
                    load(CW[:, 0, :], pick("dcn_w"))

            def store_parts():
                for i in range(CONVS):
                    sp.wait_ge(split_done, i + 3)
                    for yx in range(2):
                        rows = slice(OFFS // 2 * yx, OFFS // 2 * (yx + 1))
                        dst = off_store[yx].rearrange("s k i x -> (k i) s x")[:, :, CONV_PX * i:CONV_PX * (i + 1)]
                        sp.dma_start(dst, PART[rows, i % 2, :, :]).then_inc(parts_stored[i % 2], 16)
                for par in range(2):
                    sp.wait_ge(parts_stored[par], 16 * 2 * CONVS // 2)

            def stage(sh, c, par):
                at = (c if sh.kind == 0 else c // 2) * BIG
                for yx in range(2):
                    src = off_store[yx].rearrange("s k i x -> (s k) i x")[:, :, bass.ds(at, BIG)]
                    dst = OC[CH * yx:CH * yx + SPLIT_ROWS, par, :].rearrange("p (i x) -> p i x", i=IMG)
                    sp.dma_start(dst, src).then_inc(oc_full[par], 16)

            def body_of(sh):
                coord_last = sh.slot["coord", len(sh.groups) - 1]

                def body(c, par, first, last):
                    if first:
                        stage(sh, 0, 0)
                        stage(sh, 1, 1)
                    elif not last:
                        sp.wait_ge(ring_full, (c - 1) * sh.uses + coord_last + 1)
                        stage(sh, c + 1, 1 - par)

                chunk_loop(sp, sh, body, lambda c: None)

            def fallback(sh):
                T = turns(sh)
                with sp.Fori(0, sh.chunks) as c:
                    sp.wait_ge(turn, turn_base(T, c) - 2)
                    stage(sh, c, 0)
                    for yx in range(2):
                        row = CH * yx + ROW_BLOCK
                        sp.dma_start(OC[row:row + 1, 0, :],
                                     t["blocks"][yx:yx + 1, bass.ds(c // 2 * IMG * BIG, IMG * BIG)]).then_inc(oc_full[0], 16)
                    sp.wait_ge(oc_full[0], 16 * 4 * (c + 1))
                    sp.sem_inc(turn, 1)
                wait_alone(sp, turn, turn_base(T, sh.chunks) - 2)
                sp.dma_start(OC[:, :, :].rearrange("p a b -> p (a b)"), t["coords"]).then_inc(oc_full[0], 16)
                sp.wait_ge(oc_full[0], 16 * (4 * sh.chunks + 1))

            def step(layer, group, bar_count, final):
                if final:
                    sp.dma_start(h_view(1, 0, 0, SIDE, SIDE),
                                 gn_store[bass.ds(group, 1)].rearrange("a p (r c) -> p (a r) c", c=SIDE)).then_inc(final_loaded, 16)
                    sp.wait_ge(copied, 1)
                    sp.dma_start(X[:, bass.ds(group * XSIZE, PIX)],
                                 t["x"][bass.ds(group * IMG, IMG)].rearrange("b c h w -> (b c) (h w)")).then_inc(final_loaded, 16)
                    wait_alone(sp, final_loaded, 32 * group + 32)
                store_parts()
                sampling(sp, bar_count, final, body_of, fallback)
                if final:
                    sp.dma_start(t["out"][bass.ds(group * IMG, IMG)].rearrange("b c h w -> (b c) (h w)"),
                                 X[:, bass.ds(group * XSIZE, PIX)]).then_inc(out_stored, 16)

            each_step(sp, layer_start, step)
            sp.wait_ge(out_stored, 16 * GROUPS)

        N_LOADS = 4
        N_FINAL_LOADS = 5

        def wait_weights(eng, layer, final):
            if final:
                eng.wait_ge(weights_loaded, 16 * (LAYERS * N_LOADS + N_FINAL_LOADS))
            else:
                wait_alone(eng, weights_loaded, 16 * N_LOADS * (layer + 1))

        @block.tensor
        def _(pe):
            def layer_start(layer, final):
                wait_weights(pe, layer, final)

            def first_conv(group):
                for i in range(CONVS):
                    pe.wait_ge(conv_free, i + 1)
                    for k in range(TAPS):
                        mm = nc.tensor.matmul(P[:, i % 2, :], DW[:, 128 * k:128 * (k + 1)],
                                              x_view(group, i * CONV_ROWS + k // 3, k % 3, CONV_ROWS, SIDE),
                                              start=k == 0, stop=k == TAPS - 1)
                    mm.then_inc(conv_full, 1)

            def offset_conv(sources):
                for i in range(CONVS):
                    pe.wait_ge(off_free, i + 1)
                    for s in range(sources):
                        for k in range(TAPS):
                            mm = nc.tensor.matmul(P[0:OFFS, 3 + i % 2, :], OW[:, s, OFFS * k:OFFS * (k + 1)],
                                                  h_view(s, i * CONV_ROWS + k // 3 - 1, k % 3 - 1, CONV_ROWS, SIDE),
                                                  start=s == 0 and k == 0, stop=s == sources - 1 and k == TAPS - 1)
                    mm.then_inc(off_full, 1)

            def coord(sh, j, slot, par):
                for i in range(sh.groups[j]):
                    img, tap = divmod(sh.starts[j] + i, TAPS)
                    for n in range(sh.tiles + 1):
                        yx = 1 if n == sh.tiles else 0
                        table = n if sh.kind == 0 else 2 + n
                        off = OC[:, par, BIG * img:BIG * (img + 1)]
                        if sh.kind:
                            off = off.rearrange("p (r h c) -> p h r c", r=BLK, h=2)[:, coord_half[0]]
                        mm = nc.tensor.matmul(bank(sh, slot, n)[0:sh.npos, i * sh.px:(i + 1) * sh.px],
                                              SEL[:, table, 128 * tap:128 * tap + sh.npos],
                                              off, start=True, stop=True)
                return mm

            coord_half = [0]

            def sample(sh, source, first, blocks, par, half, tile_of):
                for w in range(blocks):
                    out = PS[:, half + w // 2, 144 * (w % 2):144 * (w % 2) + 144]
                    for n in range(sh.tiles):
                        a = A[0:sh.npos, par, n * 36 * sh.px:(n + 1) * 36 * sh.px].rearrange(
                            "p (k y x) -> p k y x", k=36, y=BLK)
                        for img in range(IMG):
                            q = slice(CH * img, CH * (img + 1))
                            mm = nc.tensor.matmul(
                                out[q].rearrange("p (k y x) -> p k y x", k=TAPS, y=BLK),
                                VT[0:sh.npos, tile_of(source, first + w, n), q],
                                a[:, TAPS * img:TAPS * (img + 1), :, BLK * (first + w):BLK * (first + w + 1)],
                                start=n == 0, stop=n == sh.tiles - 1)
                return mm

            def deform(sh, third, thirds=1):
                products = [(s, k) for s in range(sh.sources) for k in range(TAPS)]
                count = len(products) // thirds
                for n in range(third * count, (third + 1) * count):
                    s, k = products[n]
                    rhs = smp_px(s, 0, sh.blocks).rearrange("p (w k a) -> p w k a", k=TAPS, a=BPIX)[:, :, k, :]
                    mm = nc.tensor.matmul(PS[:, 0, 0:sh.px], CW[:, s, 128 * k:128 * (k + 1)], rhs,
                                          start=n == 0, stop=n == len(products) - 1)
                return mm

            def transpose(sh, slot, i, n, column):
                return nc.tensor.transpose(bank(sh, slot, column // 4)[0:sh.npos, 128 * (column % 4):128 * (column % 4) + 128],
                                           win_view(sh, i)[:, n * sh.npos:(n + 1) * sh.npos], IDENT[:, :])

            def body_of(sh):
                tile_of = lambda s, w, n: (s * sh.blocks + w) * sh.tiles + n

                def use(c, name, j=0):
                    n = sh.slot[name, j]
                    pe.wait_ge(ring_free, c * sh.uses + n + 1 + RING - sh.depth)
                    return n % sh.depth

                def part(c, n, par):
                    pe.wait_ge(hats_full, (c + 1) * len(sh.groups))
                    pe.wait_ge(smp_free, c * sh.ps_uses + max(n - 1, 0) + 2)
                    sample(sh, *sh.parts[n], 2, par, n % 2, tile_of).then_inc(smp_full, 1)

                def body(c, par, first, last):
                    pe.wait_ge(oc_full[par], 16 * 2 * (c // 2 + 1))
                    coord_half[0] = par
                    for name, j in sh.order:
                        if name == "coord":
                            slot = use(c, name, j)
                            coord(sh, j, slot, par).then_inc(ring_full, 1)
                            if not first:
                                for n in sh.after.get(j, []):
                                    part(c - 1, n, 1 - par)
                        else:
                            first_window, count = sh.windows[j]
                            pe.wait_ge(win_full, c * sh.jobs + first_window // 4 + 1)
                            slot = use(c, name, j)
                            for i in range(count):
                                half = par if sh.jobs == 1 else first_window // 4 % 2
                                for n in range(sh.tiles):
                                    mm = transpose(sh, slot, (first_window + i) % 4 + 4 * half, n, i * sh.tiles + n)
                            mm.then_inc(ring_full, 1)
                        if not first and (name, j) in sh.thirds:
                            third = sh.thirds.index((name, j))
                            if third == 0:
                                pe.wait_ge(smp_free, (c - 1) * sh.ps_uses + len(sh.parts) + 2)
                            mm = deform(sh, third, 3)
                            if third == 2:
                                mm.then_inc(smp_full, 1)

                def tail(c):
                    pe.wait_ge(ring_free, c * sh.uses + RING)
                    for n in range(len(sh.parts)):
                        part(c - 1, n, 1)
                    pe.wait_ge(smp_free, (c - 1) * sh.ps_uses + len(sh.parts) + 2)
                    deform(sh, 0).then_inc(smp_full, 1)

                chunk_loop(pe, sh, body, tail)

            def fallback(sh):
                T = turns(sh)

                def chunk(c, par):
                    coord_half[0] = par
                    with pe.Fori(0, WINDOWS) as p:
                        base = turn_base(T, c, p)
                        pe.wait_ge(turn, base + T["transpose"])
                        for s in range(sh.sources):
                            for n in range(sh.tiles):
                                mm = transpose(sh, 0, s, n, s * sh.tiles + n)
                        mm.then_inc(turn, 1)
                        for j in range(len(sh.groups)):
                            pe.wait_ge(turn, base + T["coord", j])
                            coord(sh, j, 0, 0).then_inc(turn, 1)
                        for s in range(sh.sources):
                            pe.wait_ge(turn, base + T["sample", s])
                            sample(sh, s, 0, 4, 0, 0, lambda s, w, n: s * sh.tiles + n).then_inc(turn, 1)
                    pe.wait_ge(turn, turn_base(T, c, WINDOWS))
                    deform_sum(sh).then_inc(turn, 1)

                def deform_sum(sh):
                    for s in range(sh.sources):
                        for k in range(TAPS):
                            rhs = smp_px(s, 4, 4).rearrange("p (w k a) -> p w k a", k=TAPS, a=BPIX)[:, :, k, :]
                            mm = nc.tensor.matmul(P[:, 0, 0:sh.px], CW[:, s, 128 * k:128 * (k + 1)], rhs,
                                                  start=s == 0 and k == 0, stop=s == sh.sources - 1 and k == TAPS - 1)
                    return mm

                with pe.Fori(0, sh.chunks // 2) as pair:
                    chunk(2 * pair, 0)
                    chunk(2 * pair + 1, 1)

            def step(layer, group, bar_count, final):
                if not final:
                    first_conv(group)
                    pe.wait_ge(conv_free, CONVS + 2)
                else:
                    pe.wait_ge(copied, 1)
                    wait_alone(pe, final_loaded, 32 * group + 32)
                offset_conv(2 if final else 1)
                sampling(pe, bar_count, final, body_of, fallback)

            each_step(pe, layer_start, step)

        @block.scalar
        def _(act):
            for g in range(GROUPS):
                act.wait_ge(gn_step, 1 + 4 * g + 3)
                nc.scalar.activation(MX[:, 4 * g + 2:4 * g + 3], MX[:, 4 * g + 1:4 * g + 2], ACT.Sqrt).then_inc(gn_root, 1)

            def layer_start(layer, final):
                wait_weights(act, layer, final)

            def raster(sh, sums):
                return sums[:, 0:sh.px].rearrange("p (w y x) -> p y w x", w=sh.blocks, y=BLK)

            def tmp_view(sh):
                return TMP[:, 0:sh.px].rearrange("p (y w x) -> p y w x", y=BLK, w=sh.blocks)

            def body_of(sh, final):
                ngr = len(sh.groups)

                def out_act(c):
                    act.wait_ge(smp_full, (c + 1) * sh.ps_uses + 2)
                    act.wait_ge(res_done, c + 1)
                    nc.scalar.activation(tmp_view(sh), raster(sh, PS[:, 0, :]), ACT.Identity if final else ACT.Relu,
                                         bias=BIAS[:, 1:2]).then_inc(smp_free, 1)

                def read_part(c, n):
                    s, w = sh.parts[n]
                    act.wait_ge(smp_full, c * sh.ps_uses + n + 3)
                    nc.scalar.activation(smp_px(s, w, 2), PS[:, n % 2, 0:288], ACT.Copy).then_inc(smp_free, 1)

                def body(c, par, first, last):
                    for n, (name, j) in enumerate(sh.order):
                        act.wait_ge(ring_full, c * sh.uses + n + 1)
                        b0 = n % sh.depth * sh.banks
                        if name == "coord":
                            if not (first and j < AXY_BUFS):
                                act.wait_ge(hats_full, c * ngr + j + 1 - AXY_BUFS)
                            size = sh.groups[j] * sh.px
                            nc.scalar.activation(distances(sh, j)[:, :, 0:size], P[0:sh.npos, b0:b0 + sh.banks, 0:size],
                                                 ACT.Abs).then_inc(ring_free, 1)
                            if not first:
                                for part in sh.after.get(j, []):
                                    read_part(c - 1, part)
                        else:
                            tile, count = (sh.tiles * v for v in sh.windows[j])
                            vt = VT[0:sh.npos, tile:tile + count, :].rearrange("p a b -> p (a b)")
                            if count <= 4:
                                src = P[0:sh.npos, b0, 0:128 * count]
                            else:
                                src = P[0:sh.npos, b0:b0 + 2, :].rearrange("p a b -> p (a b)")
                            nc.scalar.activation(vt, src, ACT.Copy).then_inc(ring_free, 1)
                    if not first:
                        out_act(c - 1)

                def tail(c):
                    for n in range(len(sh.parts)):
                        read_part(c - 1, n)
                    out_act(c - 1)

                chunk_loop(act, sh, body, tail)

            def fallback_of(sh, final):
                T = turns(sh)
                with act.Fori(0, sh.chunks) as c:
                    with act.Fori(0, WINDOWS) as p:
                        base = turn_base(T, c, p)
                        wait_alone(act, turn, base + T["keep"])
                        count = sh.sources * sh.tiles
                        nc.scalar.activation(VT[:, 0:count, :], P[:, 0, 0:128 * count].rearrange(
                            "p (a b) -> p a b", b=128), ACT.Copy).then_inc(turn, 1)
                        for j in range(len(sh.groups)):
                            wait_alone(act, turn, base + T["abs", j])
                            size = sh.groups[j] * sh.px
                            buf = AXY[:, 0, 0:3 * sh.bank].rearrange("p (n a) -> p n a", n=3)
                            nc.scalar.activation(buf[:, 0:2, 0:size], P[:, 0:2, 0:size], ACT.Abs,
                                                 bias=CONST[:, bass.ds(LAYERS + 1 + p // 4, 1)])
                            nc.scalar.activation(buf[:, 2, 0:size], P[:, 2, 0:size], ACT.Abs,
                                                 bias=CONST[:, bass.ds(LAYERS + 1 + p % 4, 1)]).then_inc(turn, 1)
                        for s in range(sh.sources):
                            wait_alone(act, turn, base + T["read", s])
                            nc.scalar.activation(smp_px(s, 0, 4).rearrange("p (a b) -> p a b", a=2), PS[:, :, 0:288],
                                                 ACT.Copy).then_inc(turn, 1)
                    wait_alone(act, turn, turn_base(T, c, WINDOWS) + 1)
                    nc.scalar.activation(tmp_view(sh), raster(sh, P[:, 0, :]), ACT.Identity if final else ACT.Relu,
                                         bias=BIAS[:, 1:2]).then_inc(turn, 1)

            def step(layer, group, bar_count, final):
                if not final:
                    for i in range(CONVS):
                        act.wait_ge(conv_full, i + 1)
                        nc.scalar.activation(h_view(0, i * CONV_ROWS, 0, CONV_ROWS, SIDE),
                                             P[:, i % 2, :].rearrange("p (r c) -> p r c", c=SIDE), ACT.Relu,
                                             bias=BIAS[:, 0:1]).then_inc(conv_free, 1)
                sampling(act, bar_count, final, lambda sh: body_of(sh, final), lambda sh: fallback_of(sh, final))

            each_step(act, layer_start, step)

        @block.vector
        def _(dve):
            nc.vector.memset(X[:, :], 0.0).then_inc(gn_step, 1)
            stats = AXY[:, 0, 0:48].rearrange("p (a b) -> p a b", b=6)
            for g in range(GROUPS):
                done = 1 + 4 * g
                dve.wait_ge(x_loaded[g], 16)
                dve.wait_ge(gn_step, done)
                for i in range(8):
                    last = nc.vector.bn_stats(stats[:, i, :], A[:, g, 512 * i:512 * (i + 1)])
                last.then_inc(gn_step, 1)
                dve.wait_ge(gn_step, done + 1)
                nc.vector.bn_aggr(MX[:, 4 * g:4 * g + 2], stats).then_inc(gn_step, 1)
                dve.wait_ge(gn_step, done + 2)
                nc.vector.tensor_scalar_add(MX[:, 4 * g + 1:4 * g + 2], MX[:, 4 * g + 1:4 * g + 2], EPS).then_inc(gn_step, 1)
                dve.wait_ge(gn_root, g + 1)
                nc.vector.reciprocal(MX[:, 4 * g + 3:4 * g + 4], MX[:, 4 * g + 2:4 * g + 3]).then_inc(gn_step, 1)
                dve.wait_ge(gn_step, done + 4)
                nc.vector.tensor_scalar(x_view(g, 1, 1, SIDE, SIDE), A[:, g, 0:PIX].rearrange("p (r c) -> p r c", c=SIDE),
                                        MX[:, 4 * g:4 * g + 1], MX[:, 4 * g + 3:4 * g + 4], ALU.subtract,
                                        ALU.mult).then_inc(gn_done, 1)
            dve.wait_ge(loaded, 64)

            def layer_start(layer, final):
                wait_weights(dve, layer, final)

            def residual(sh, layer, group, c, final):
                row, col = place(sh, c)
                tmp = TMP[:, 0:sh.px].rearrange("p (r c) -> p r c", r=BLK)
                if final:
                    dst = out_view(group, row, col, sh.cols)
                    flag = CONST[:, LAYERS:LAYERS + 1]
                else:
                    dst = x_view(group, row + 1, col + 1, BLK, sh.cols)
                    flag = CONST[:, bass.ds(layer, 1)]
                return nc.vector.scalar_tensor_tensor(dst, dst, flag, tmp, ALU.mult, ALU.add)

            def product(sh, j, buf, par):
                size = sh.groups[j] * sh.px
                a = A[0:sh.npos, par, 0:sh.tiles * 36 * sh.px].rearrange("p (n a) -> p n a", n=sh.tiles)
                a = a[:, :, sh.starts[j] * sh.px:sh.starts[j] * sh.px + size]
                hx = buf[:, sh.tiles:sh.tiles + 1, 0:size]
                if sh.tiles > 1:
                    hx = hx.broadcast_to([sh.npos, sh.tiles, size])
                return nc.vector.tensor_tensor(a, buf[:, 0:sh.tiles, 0:size], hx, ALU.mult)

            def body_of(sh, layer, group, final):
                ngr = len(sh.groups)

                def clamp(c, j):
                    size = sh.groups[j] * sh.px
                    buf = distances(sh, j)[:, :, 0:size]
                    dve.wait_ge(ring_free, c * sh.uses + sh.slot["coord", j] + 1 + RING)
                    nc.vector.tensor_scalar(buf, buf, 1.0, 1.0, ALU.min, ALU.subtract).then_inc(clamp_done, 1)

                def body(c, par, first, last):
                    clamp(c, 0)
                    for j in range(ngr):
                        if j + 1 < ngr:
                            clamp(c, j + 1)
                        dve.wait_ge(clamp_done, c * ngr + j + 1)
                        if not first and j == 0:
                            dve.wait_ge(smp_full, (c - 1) * sh.ps_uses + 1)
                        product(sh, j, distances(sh, j), par).then_inc(hats_full, 1)
                    if not first:
                        dve.wait_ge(smp_free, c * sh.ps_uses + 2)
                        residual(sh, layer, group, c - 1, final).then_inc(res_done, 1)

                def tail(c):
                    dve.wait_ge(smp_free, c * sh.ps_uses + 2)
                    residual(sh, layer, group, c - 1, final).then_inc(res_done, 1)

                chunk_loop(dve, sh, body, tail)

            def fallback_of(sh, layer, group, final):
                T = turns(sh)
                with dve.Fori(0, sh.chunks) as c:
                    dve.wait_ge(turn, turn_base(T, c) - 1)
                    for s in range(sh.sources):
                        mm = nc.vector.memset(smp_px(s, 4, 4), 0.0)
                    mm.then_inc(turn, 1)
                    with dve.Fori(0, WINDOWS) as p:
                        base = turn_base(T, c, p)
                        for j in range(len(sh.groups)):
                            size = sh.groups[j] * sh.px
                            buf = AXY[:, 0, 0:3 * sh.bank].rearrange("p (n a) -> p n a", n=3)
                            dve.wait_ge(turn, base + T["clamp", j])
                            nc.vector.tensor_scalar(buf[:, :, 0:size], buf[:, :, 0:size], 1.0, 1.0, ALU.min,
                                                    ALU.subtract).then_inc(turn, 1)
                            dve.wait_ge(turn, base + T["product", j])
                            product(sh, j, buf, 0).then_inc(turn, 1)
                        for s in range(sh.sources):
                            dve.wait_ge(turn, base + T["add", s])
                            nc.vector.tensor_tensor(smp_px(s, 4, 4), smp_px(s, 4, 4), smp_px(s, 0, 4),
                                                    ALU.add).then_inc(turn, 1)
                    dve.wait_ge(turn, turn_base(T, c, WINDOWS) + 2)
                    residual(sh, layer, group, c, final).then_inc(turn, 1)

            def step(layer, group, bar_count, final):
                if final:
                    nc.vector.tensor_copy(h_view(0, 0, 0, SIDE, SIDE), x_view(group, 1, 1, SIDE, SIDE)).then_inc(copied, 1)
                nc.vector.memset(MX[:, :], 0.0).then_inc(flag_step, 1)
                dve.wait_ge(flag_step, 1)
                for i in range(CONVS):
                    dve.wait_ge(off_full, i + 1)
                    dve.wait_ge(split_done, i + 1)
                    dve.wait_ge(max_done, i + 1)
                    for strip in range(CONV_ROWS // BLK):
                        src = P[0:OFFS, 3 + i % 2, 2 * BIG * strip:2 * BIG * (strip + 1)]
                        dst = FOFF[:, i % 2, 2 * BIG * strip:2 * BIG * (strip + 1)]
                        fo = nc.vector.tensor_scalar(dst.rearrange("p (h r c) -> p r h c", h=2, r=BLK),
                                                     src.rearrange("p (r h c) -> p r h c", h=2, r=BLK),
                                                     BIAS[0:OFFS, 2:3], None, ALU.add)
                    fo.then_inc(off_free, 1)
                    dve.wait_ge(off_free, i + 3)
                    nc.vector.tensor_reduce(MX[0:OFFS, i:i + 1], FOFF[:, i % 2, :], AX.X, ALU.max,
                                            apply_absolute_value=True).then_inc(max_done, 1)
                dve.wait_ge(max_done, CONVS + 2)
                nc.vector.tensor_reduce(MX[:, CONVS:CONVS + 1], MX[:, 0:CONVS], AX.X, ALU.max).then_inc(flag_step, 1)
                dve.wait_ge(flag_step, 3)
                nc.vector.tensor_scalar(MX[:, CONVS + 2:CONVS + 3], MX[:, CONVS + 1:CONVS + 2], BOUND0, None, ALU.is_ge).then_inc(flag_step, 1)
                nc.vector.tensor_scalar(MX[:, CONVS + 3:CONVS + 4], MX[:, CONVS + 1:CONVS + 2], BOUND1, None, ALU.is_ge).then_inc(flag_step, 1)
                dve.wait_ge(flag_step, 5)
                nc.vector.tensor_tensor(FLAG[:, :], MX[:, CONVS + 2:CONVS + 3], MX[:, CONVS + 3:CONVS + 4], ALU.add).then_inc(flag_step, 1)
                sampling(dve, bar_count, final, lambda sh: body_of(sh, layer, group, final),
                         lambda sh: fallback_of(sh, layer, group, final))

            each_step(dve, layer_start, step)

        @block.gpsimd
        def _(pool):
            nc.gpsimd.memset(H[:, :], 0.0)

            def body_of(sh):
                def fill(c, j, half):
                    row, col = place(sh, c)
                    for i in range(4):
                        s, w = divmod(4 * j + i, sh.blocks)
                        cp = nc.gpsimd.tensor_copy(
                            win_view(sh, i + 4 * half).rearrange("p (r c) -> p r c", c=sh.win),
                            h_view(s, row - sh.margin, col + BLK * w - sh.margin, sh.win, sh.win))
                    cp.then_inc(win_full, 1)

                def body(c, par, first, last):
                    if sh.jobs == 1:
                        if first:
                            fill(0, 0, 0)
                            fill(1, 0, 1)
                        elif not last:
                            pool.wait_ge(ring_full, (c - 1) * sh.uses + sh.job_last[0] + 1)
                            fill(c + 1, 0, 1 - par)
                        return
                    for j in range(sh.jobs):
                        if j >= 2:
                            pool.wait_ge(ring_full, c * sh.uses + sh.job_last[j - 2] + 1)
                        elif not first:
                            pool.wait_ge(ring_full, (c - 1) * sh.uses + sh.job_last[sh.jobs + j - 2] + 1)
                        fill(c, j, j % 2)

                chunk_loop(pool, sh, body, lambda c: None)

            def fallback(sh):
                T = turns(sh)
                with pool.Fori(0, sh.chunks) as c:
                    with pool.Fori(0, WINDOWS) as p:
                        pool.wait_ge(turn, turn_base(T, c, p) + T["window"])
                        for s in range(sh.sources):
                            cp = nc.gpsimd.tensor_copy(win_view(sh, s).rearrange("p (r c) -> p r c", c=sh.win),
                                                       h_view(s, (p // 4) * 16, (p % 4) * 16, sh.win, sh.win))
                        cp.then_inc(turn, 1)

            def step(layer, group, bar_count, final):
                for i in range(CONVS):
                    foff, part = FOFF[:, i % 2, :], PART[:, i % 2]
                    pool.wait_ge(off_free, i + 3)
                    if i >= 2:
                        pool.wait_ge(parts_stored[i % 2], 16 * 2 * (i // 2))
                    nc.gpsimd.tensor_copy(part[:, 0, :], foff).then_inc(split_step, 1)
                    pool.wait_ge(split_step, 3 * i + 1)
                    nc.gpsimd.tensor_tensor(REST[:, :], foff, part[:, 0, :], ALU.subtract).then_inc(split_step, 1)
                    pool.wait_ge(split_step, 3 * i + 2)
                    nc.gpsimd.tensor_copy(part[:, 1, :], REST[:, :]).then_inc(split_step, 1)
                    pool.wait_ge(split_step, 3 * i + 3)
                    nc.gpsimd.tensor_tensor(part[:, 2, :], REST[:, :], part[:, 1, :], ALU.subtract).then_inc(split_done, 1)
                    pool.wait_ge(split_done, i + 3)
                pool.wait_ge(flag_step, 2)
                nc.gpsimd.partition_all_reduce(MX[:, CONVS + 1:CONVS + 2], MX[:, CONVS:CONVS + 1], 128,
                                               bass.bass_isa.ReduceOp.max).then_inc(flag_step, 1)
                sampling(pool, bar_count, final, body_of, fallback, clears=True)

            each_step(pool, lambda layer, final: None, step, clears=True)


def _tables():
    npos = {0: 100, 1: 128}
    sel = np.zeros((128, 5, TAPS, 128), np.float32)
    tables = [(0, 0, 0), (0, 1, 0), (1, 0, 0), (1, 0, 1), (1, 1, 0)]
    for n, (kind, yx, tile) in enumerate(tables):
        win, rows, margin = (10, 10, 3) if kind == 0 else (16, 8, 6)
        q = CH * yx
        for k in range(TAPS):
            for s in range(PARTS):
                sel[q + s * TAPS + k, n, k, :] = 1.0
            pos = np.arange(npos[kind])
            at = pos % win if yx else pos // win + rows * tile
            shift = (k % 3 if yx else k // 3) - 1
            sel[q + ROW_ONE, n, k, :npos[kind]] = shift + margin - at
            sel[q + ROW_PIXEL, n, k, :] = 1.0
            sel[q + ROW_BLOCK, n, k, :] = 1.0
    pixels = np.arange(BIG)
    coords = np.zeros((128, 2, IMG, BIG), np.float32)
    for yx in range(2):
        coords[CH * yx + ROW_ONE] = 1.0
        coords[CH * yx + ROW_PIXEL] = pixels % BLK if yx else pixels // 32
    blocks = np.zeros((2, NBIG, IMG, BIG), np.float32)
    for c in range(NBIG):
        blocks[0, c] = c // 2 * BLK
        blocks[1, c] = c % 2 * 32 + pixels % 32 // BLK * BLK
    consts = np.zeros((128, 9), np.float32)
    consts[:, 0:5] = [0.0, 1.0, 1.0, 0.0, 1.0]
    consts[:, 5:9] = -6.0 - 16.0 * np.arange(4)
    return dict(sel=sel.reshape(128, -1), coords=coords.reshape(128, -1), blocks=blocks.reshape(2, -1)), consts


def kernel(**inputs):
    import concourse.bacc as bacc
    import ml_dtypes
    from concourse.bass_utils import run_bass_kernel_spmd

    a = {k.replace("L0_conv_", ""): np.asarray(v) for k, v in inputs.items()}
    L = LAYERS

    def diagonal(w):
        full = np.zeros((IMG, CH, TAPS, IMG, CH), w.dtype)
        for i in range(IMG):
            full[i, :, :, i] = w
        return full.reshape(128, TAPS * 128)

    def diagonal_off(w):
        w = w.reshape(TAPS, 2, CH, TAPS)
        full = np.zeros((IMG, CH, TAPS, 2, TAPS, IMG), w.dtype)
        for i in range(IMG):
            full[i, :, :, :, :, i] = w.transpose(2, 3, 1, 0)
        return full.reshape(128, TAPS * OFFS)

    dc = np.stack([diagonal(w[:, :, ::-1, ::-1].reshape(CH, CH, TAPS).transpose(0, 2, 1)) for w in a["deconv_w"]])
    dcn = np.stack([diagonal(w.reshape(CH, CH, TAPS).transpose(1, 2, 0)) for w in a["dcn_w"]])
    off = np.stack([diagonal_off(w.reshape(2 * TAPS, CH, TAPS)) for w in a["off_w"]])
    fin_off, fin_dcn = a["fin_off_w"], a["fin_dcn_w"]
    fin_off = np.stack([diagonal_off(fin_off[:, CH * s:CH * (s + 1)].reshape(2 * TAPS, CH, TAPS)) for s in range(2)])
    fin_dcn = np.stack([diagonal(fin_dcn[:, CH * s:CH * (s + 1)].reshape(CH, CH, TAPS).transpose(1, 2, 0))
                        for s in range(2)])
    bias = np.zeros((L + 1, 128, 3), np.float32)
    for l in range(L + 1):
        dcn_b = a["dcn_b"][l] if l < L else a["fin_dcn_b"]
        off_b = a["off_b"][l] if l < L else a["fin_off_b"]
        if l < L:
            bias[l, :, 0] = np.tile(a["deconv_b"][l], IMG)
        bias[l, :, 1] = np.tile(dcn_b, IMG)
        bias[l, :OFFS, 2] = np.repeat(off_b.reshape(TAPS, 2).T.reshape(-1), IMG)
    tables, consts = _tables()
    arrays = {"x": a["x"], "dc_w": dc, "off_w": off, "dcn_w": dcn, "fin_off_w": fin_off, "fin_dcn_w": fin_dcn, "bias": bias,
              "consts": consts, "ident": np.eye(128, dtype=np.float32)}
    for name, table in tables.items():
        arrays[name] = table.astype(ml_dtypes.bfloat16)
    nc = bacc.Bacc("TRN2", target_bir_lowering=False, num_devices=1)
    feed, t = {}, {}
    for name, v in arrays.items():
        v = np.ascontiguousarray(v)
        feed[f"{name}_dram"] = v
        t[name] = nc.dram_tensor(f"{name}_dram", v.shape, mybir.dt.from_np(v.dtype), kind="ExternalInput").ap()
    t["out"] = nc.dram_tensor("out_dram", a["x"].shape, F32, kind="ExternalOutput").ap()
    build(nc, t)
    return run_bass_kernel_spmd(nc, [feed], core_ids=[0]).results[0]["out_dram"]
```
